# Optimizing a Trainium2 kernel written in Bass

```python
import numpy as np
import jax
import jax.numpy as jnp

def _softmax(x, axis=-1):
    return jax.nn.softmax(x, axis=axis)

def _gelu(x):
    return jax.nn.gelu(x, approximate=True)

def _silu(x):
    return jax.nn.silu(x)

def _sigmoid(x):
    return jax.nn.sigmoid(x)

def _layernorm(x, axis=-1, eps=1e-05):
    m = jnp.mean(x, axis=axis, keepdims=True)
    v = jnp.var(x, axis=axis, keepdims=True)
    return (x - m) / jnp.sqrt(v + eps)

def _scatter_add(tgt, idx, src, axis=0):
    return tgt.at[idx].add(src)

def _segment_sum(src, seg, n):
    return jax.ops.segment_sum(src, seg, n)
kernel_name = 'mk_adj_ffn_d1_adj_r2_a4f6fe'

def setup_inputs(seed: int=0):
    np.random.seed(seed)
    _w = jnp.asarray

    def _rec_inputs():
        import jax
        import jax.numpy as jnp
        _gk = jax.random.key(seed)
        x = -0.0003929 + 0.9999 * jax.random.normal(jax.random.fold_in(_gk, 1), (32, 256, 128), jnp.float32)
        _w = (1.0 + jnp.arange(256, dtype=jnp.float32)) ** (-0.5)
        _w = _w / _w.mean()
        _pij = jnp.clip(0.015625 * _w[:, None] * _w[None, :], 0.0, 1.0)
        _a = jax.random.uniform(jax.random.fold_in(_gk, 2), (256, 256)) < _pij
        _a = jnp.logical_or(_a, jnp.swapaxes(_a, -1, -2))
        _a = jnp.logical_or(_a, jnp.eye(256, dtype=bool))
        _af = _a.astype(jnp.float32)
        _af = _af * jax.random.uniform(jax.random.fold_in(_gk, 3), (256, 256), jnp.float32, 0.05, 1)
        adj = _af
        return (x, adj)
    x, adj = _rec_inputs()

    def _L0_gnn_setup():
        import jax, jax.numpy as jnp
        import numpy as np
        EPS = 1e-05

        def _batchnorm(x, gamma, beta):
            mu = jnp.mean(x, axis=0)
            var = jnp.var(x, axis=0)
            return (x - mu) * jax.lax.rsqrt(var + EPS) * gamma + beta
        key = jax.random.key(seed)
        ks = jax.random.split(key, 4)
        b, n, d, h, o = (32, 1024, 128, 256, 128)
        features = jax.random.normal(ks[0], (b, n, d), dtype=jnp.float32)
        A = jax.random.uniform(ks[1], (n, n), dtype=jnp.float32)
        lim1 = float(np.sqrt(6.0 / (d + h)))
        W1 = jax.random.uniform(ks[2], (h, d), minval=-lim1, maxval=lim1, dtype=jnp.float32)
        b1 = jnp.zeros((h,), jnp.float32)
        lim2 = float(np.sqrt(6.0 / (h + o)))
        W2 = jax.random.uniform(ks[3], (o, h), minval=-lim2, maxval=lim2, dtype=jnp.float32)
        b2 = jnp.zeros((o,), jnp.float32)
        g1 = jnp.ones((h,), jnp.float32)
        be1 = jnp.zeros((h,), jnp.float32)
        g2 = jnp.ones((o,), jnp.float32)
        be2 = jnp.zeros((o,), jnp.float32)
        return {'features': features, 'A': A, 'W1': W1, 'b1': b1, 'g1': g1, 'be1': be1, 'W2': W2, 'b2': b2, 'g2': g2, 'be2': be2}
    _L0_gnn_all = _L0_gnn_setup()
    _L0_gnn_in = {k: v for k, v in _L0_gnn_all.items() if k in ('W1', 'b1', 'g1', 'be1', 'W2', 'b2', 'g2', 'be2')}
    del _L0_gnn_all

    def _L0_ffn_setup():
        import jax, jax.numpy as jnp
        import numpy as np
        B, S, D, E, H, K = (4, 2048, 128, 8, 256, 2)
        key = jax.random.key(seed)
        ks = jax.random.split(key, 6)
        x = jax.random.normal(ks[0], (B, S, D), jnp.float32)
        Wg = jax.random.normal(ks[1], (D, E), jnp.float32) * 0.02
        bg = jnp.zeros((E,), jnp.float32)
        W1 = jax.random.normal(ks[2], (E, D, H), jnp.float32) * 0.02
        b1 = jnp.zeros((E, H), jnp.float32)
        W2 = jax.random.normal(ks[3], (E, H, D), jnp.float32) * 0.02
        b2 = jnp.zeros((E, D), jnp.float32)
        return {'x': x, 'Wg': Wg, 'bg': bg, 'W1': W1, 'b1': b1, 'W2': W2, 'b2': b2}
    _L0_ffn_all = _L0_ffn_setup()
    _L0_ffn_in = {k: v for k, v in _L0_ffn_all.items() if k in ('Wg', 'bg', 'W1', 'b1', 'W2', 'b2')}
    del _L0_ffn_all
    return {'x': x, 'adj': adj, 'L0_gnn_W1': _L0_gnn_in['W1'], 'L0_gnn_b1': _L0_gnn_in['b1'], 'L0_gnn_g1': _L0_gnn_in['g1'], 'L0_gnn_be1': _L0_gnn_in['be1'], 'L0_gnn_W2': _L0_gnn_in['W2'], 'L0_gnn_b2': _L0_gnn_in['b2'], 'L0_gnn_g2': _L0_gnn_in['g2'], 'L0_gnn_be2': _L0_gnn_in['be2'], 'L0_ffn_Wg': _L0_ffn_in['Wg'], 'L0_ffn_bg': _L0_ffn_in['bg'], 'L0_ffn_W1': _L0_ffn_in['W1'], 'L0_ffn_b1': _L0_ffn_in['b1'], 'L0_ffn_W2': _L0_ffn_in['W2'], 'L0_ffn_b2': _L0_ffn_in['b2']}

def reference(x, adj, L0_gnn_W1, L0_gnn_b1, L0_gnn_g1, L0_gnn_be1, L0_gnn_W2, L0_gnn_b2, L0_gnn_g2, L0_gnn_be2, L0_ffn_Wg, L0_ffn_bg, L0_ffn_W1, L0_ffn_b1, L0_ffn_W2, L0_ffn_b2):
    import jax
    import jax.numpy as jnp

    def _L0_gnn_ref(features, A, W1, b1, g1, be1, W2, b2, g2, be2):
        import jax, jax.numpy as jnp
        import numpy as np
        EPS = 1e-05

        def _batchnorm(x, gamma, beta):
            mu = jnp.mean(x, axis=0)
            var = jnp.var(x, axis=0)
            return (x - mu) * jax.lax.rsqrt(var + EPS) * gamma + beta
        b, n, d = features.shape
        A_norm = A + jnp.eye(n, dtype=A.dtype)
        deg = jnp.sum(A_norm, axis=0) + jnp.sum(A_norm, axis=1) - jnp.diagonal(A_norm)
        dinv = jax.lax.rsqrt(deg)
        A_hat = A_norm * dinv[:, None] * dinv[None, :]
        agg = jnp.einsum('nm,bmd->bnd', A_hat, features)
        x = agg.reshape(-1, d)
        h = jax.nn.relu(_batchnorm(x @ W1.T + b1, g1, be1))
        out = h @ W2.T + b2
        out = _batchnorm(out, g2, be2)
        return out.reshape(b, n, -1)

    def _L0_ffn_ref(x, Wg, bg, W1, b1, W2, b2):
        import jax, jax.numpy as jnp
        import numpy as np
        B, S, D, E, H, K = (4, 2048, 128, 8, 256, 2)
        Bv, Sv, Dv = x.shape
        gate_scores = x @ Wg + bg
        _, idx = jax.lax.top_k(gate_scores, K)
        mask = jax.nn.one_hot(idx, E, dtype=x.dtype).sum(axis=-2)
        xf = x.reshape(-1, Dv)
        mf = mask.reshape(-1, E)
        h = jax.nn.gelu(jnp.einsum('td,edh->teh', xf, W1) + b1[None], approximate=False)
        y = jnp.einsum('teh,ehd->ted', h, W2) + b2[None]
        out = jnp.einsum('ted,te->td', y, mf)
        return out.reshape(Bv, Sv, Dv)
    x = x + _L0_gnn_ref(_layernorm(x, axis=-1), adj, L0_gnn_W1, L0_gnn_b1, L0_gnn_g1, L0_gnn_be1, L0_gnn_W2, L0_gnn_b2, L0_gnn_g2, L0_gnn_be2)
    x = x + _L0_ffn_ref(_layernorm(x, axis=-1), L0_ffn_Wg, L0_ffn_bg, L0_ffn_W1, L0_ffn_b1, L0_ffn_W2, L0_ffn_b2)
    return x

_drawn_inputs = setup_inputs


def setup_inputs(seed=0):
    import zlib

    import numpy as np

    out = dict(_drawn_inputs(seed))
    spreads = {'L0_gnn_b1': (0.0, 0.8),
     'L0_gnn_g1': (1.0, 0.2),
     'L0_gnn_be1': (0.0, 0.1),
     'L0_gnn_b2': (0.0, 0.8),
     'L0_gnn_g2': (1.0, 0.2),
     'L0_gnn_be2': (0.0, 0.1),
     'L0_ffn_bg': (0.0, 0.1),
     'L0_ffn_b1': (0.0, 0.489),
     'L0_ffn_b2': (0.0, 0.1)}
    factors = {}
    for name, (base, spread) in spreads.items():
        noise = np.random.default_rng([zlib.crc32(name.encode()), seed]).standard_normal(out[name].shape)
        drawn = base * np.exp(spread * noise) if base else spread * noise
        out[name] = jnp.asarray(drawn.astype(out[name].dtype))
    for name, factor in factors.items():
        out[name] = (out[name] * factor).astype(out[name].dtype)
    return out
```

```python
from contextlib import ExitStack

import concourse.bass as bass
from concourse import mybir

F32 = mybir.dt.float32
F32R = mybir.dt.float32r
BF16 = mybir.dt.bfloat16
U32 = mybir.dt.uint32
ALU = mybir.AluOpType
ACT = mybir.ActivationFunctionType
AX_X = mybir.AxisListType.X

P = 128
EPS = 1e-5


def from_zero(value):
    return max(value, 0) if isinstance(value, int) else value


def held(engine, register, value):
    if isinstance(value, int):
        return value
    engine.reg_mov(register, value)
    return register


def gnn_moe_program(nc, x, adj, gw1, gb1, gg1, gbe1, gw2, gb2, gg2, gbe2, wg, bg, fw1, fb1, fw2, fb2, out):
    B, N, D = x.shape
    H = gw1.shape[0]
    E, _, FH = fw1.shape
    KT = N // P
    HT = H // P
    FT = FH // P
    BG = 2
    G = B // BG
    T = BG * N
    J = T // P
    PAIRS = G // 2
    LOADS = 8
    assert D == P and KT == 2 and HT == 2 and FT == 2 and T == 512 and G % LOADS == 0

    x_rows = x.rearrange("b (p k) d -> p b (k d)", k=KT)
    out_rows = out.rearrange("b (p k) d -> p b (k d)", k=KT)

    with ExitStack() as ctx:
        def sb(name, shape, dt):
            return ctx.enter_context(nc.sbuf_tensor(name, shape, dt))

        def sem(name):
            return ctx.enter_context(nc.semaphore(name))

        x_sb = sb("x_sb", [P, G * J, D], F32)
        h1 = sb("h1", [P, HT, G * T], F32)
        y = h1[:, 0, :]
        spare = h1[:, 1, :]
        ident = sb("ident", [P, P], F32)
        ident_bf = sb("ident_bf", [P, P], BF16)
        ones = sb("ones", [P, 2], F32)
        minus_half = sb("minus_half", [P, J], F32)
        expert_number = sb("expert_number", [P, J, E], F32)
        zero_col = sb("zero_col", [P, 1], F32)

        adj_sb = sb("adj_sb", [P, KT, N], F32)
        eye = sb("eye", [P, KT, N], F32)
        eye_adj = sb("eye_adj", [P, KT, N], F32)
        a_t = sb("a_t", [P, KT, N], F32)
        row_sum = sb("row_sum", [P, KT], F32)
        diag = sb("diag", [P, KT], F32)
        deg = sb("deg", [P, KT], F32)
        dinv = sb("dinv", [P, KT], F32)

        NV = 3 * HT + 3 + E * FT + E
        vec_rows = sb("vec_rows", [P, P], F32)
        vec = sb("vec", [P, P], F32)
        names, at = {}, 0
        for name, rows in (("gb1", HT), ("gg1", HT), ("gbe1", HT), ("gb2", 1), ("gg2", 1), ("gbe2", 1),
                            ("fb1", E * FT), ("fb2", E)):
            names[name] = at
            at += rows
        assert at == NV

        def column(name, k=0):
            return vec[:, names[name] + k:names[name] + k + 1]

        gw1_raw = sb("gw1_raw", [P, HT, D], F32)
        gw2_raw = sb("gw2_raw", [P, H], F32)
        gw_t = sb("gw_t", [P, 2 * HT, P], F32)
        bg_sb = sb("bg_sb", [P, E], F32)
        wg_raw = sb("wg_raw", [P, E], F32)
        wg_hi = sb("wg_hi", [P, E], F32R)
        wg_lo = sb("wg_lo", [P, E], F32R)

        W1C = E * FH
        W2C = E * FT * D
        fw_raw = sb("fw_raw", [P, W1C + W2C], F32)
        fw_hi = sb("fw_hi", [P, W1C + W2C], F32R)
        fw_lo = sb("fw_lo", [P, W1C + W2C], F32R)
        mask_bc = fw_raw[:].bitcast(BF16)[:, 0:2 * E * T].rearrange("p (u e t) -> p u e t", u=2, e=E)

        def w1(part, e, f):
            return part[:, e * FH + f * P:e * FH + (f + 1) * P]

        def w2(part, e, f):
            at = W1C + (e * FT + f) * D
            return part[:, at:at + D]

        phase_buf = sb("phase_buf", [P, 4 * T], F32)
        xln = phase_buf[:, 0:2 * T].rearrange("p (u j d) -> p u j d", u=2, j=J)
        agg_t = phase_buf[:, 2 * T:4 * T].rearrange("p (u t) -> p u t", u=2)
        h_relu = phase_buf[:, :].rearrange("p (u k t) -> p u k t", u=2, k=HT)
        x_stats = sb("x_stats", [P, 2, J, 6], F32)
        x_mv = sb("x_mv", [P, 2, J, 2], F32)
        x_var = sb("x_var", [P, 2, J], F32)
        x_rstd = sb("x_rstd", [P, 2, J], F32)
        h_stats = sb("h_stats", [P, HT, G, 6], F32)
        h_mv = sb("h_mv", [P, HT, 2], F32)
        y_stats = sb("y_stats", [P, G, 6], F32)
        y_mv = sb("y_mv", [P, 2], F32)
        bn_var = sb("bn_var", [P, HT + 1], F32)
        bn_rstd = sb("bn_rstd", [P, HT + 1], F32)
        bn_scale = sb("bn_scale", [P, HT + 1], F32)
        bn_shift = sb("bn_shift", [P, HT + 1], F32)
        bn_mean_scaled = sb("bn_mean_scaled", [P, HT + 1], F32)

        at = 0

        def carve(count):
            nonlocal at
            at += count
            assert at <= G * T
            return spare[:, at - count:at]

        y_norm = carve(T)
        x_norm = carve(T).rearrange("p (j d) -> p j d", j=J)
        hid = carve(2 * FT * T).rearrange("p (r f t) -> p r f t", r=2, f=FT)
        y_masked = carve(2 * T).rearrange("p (r t) -> p r t", r=2)
        ffn_sum = carve(2 * T).rearrange("p (u t) -> p u t", u=2)
        out_sb = carve(2 * T).rearrange("p (u j d) -> p u j d", u=2, j=J)
        xt_hi = sb("xt_hi", [P, 2, T], F32R)
        xt_lo = sb("xt_lo", [P, 2, T], F32R)
        hid_hi = sb("hid_hi", [P, 2, FT, T], F32R)
        hid_lo = sb("hid_lo", [P, 2, FT, T], F32R)
        gate = sb("gate", [P, J, E], F32)
        gate_max = sb("gate_max", [P, J, 8], F32)
        gate_idx = sb("gate_idx", [P, J, 8], U32)
        picked = sb("picked", [P, 2, J, E], F32)
        mask = sb("mask", [P, E, J], BF16)
        mask_t = sb("mask_t", [E * J, P], BF16)
        mask_dram = nc.dram_tensor("mask_dram", (2, E * J, P), BF16).ap()

        psum = ctx.enter_context(nc.psum_tensor("psum", [P, 8, T], F32))
        agg_ps = psum[:, 0:2, :]
        h1_ps = psum[:, 2:6, :].rearrange("p (u k) t -> p u k t", u=2)
        y_ps = psum[:, 6:8, :]
        hid_ps = psum[:, 0:4, :].rearrange("p (r f) t -> p r f t", r=2)
        ffn_ps = psum[:, 4:6, :]
        work_a = psum[:, 6, :]
        work_b = psum[:, 7, :]

        const_ready = sem("const_ready")
        adj_loaded = sem("adj_loaded")
        vec_zeroed = sem("vec_zeroed")
        vec_loaded = sem("vec_loaded")
        gw_loaded = sem("gw_loaded")
        fw_loaded = sem("fw_loaded")
        x_load = [sem(f"x_load{i}") for i in range(LOADS)]
        x_loaded = sem("x_loaded")
        adj_step = sem("adj_step")
        deg_ready = sem("deg_ready")
        dinv_ready = sem("dinv_ready")
        col_sum_done = sem("col_sum_done")
        adj_scaled = sem("adj_scaled")
        adj_turned = sem("adj_turned")
        a_t_ready = sem("a_t_ready")
        weights_turned = sem("weights_turned")
        weights_ready = sem("weights_ready")
        wg_split = sem("wg_split")
        fw_split = sem("fw_split")
        ln_stats_step = sem("ln_stats_step")
        ln_mv_ready = sem("ln_mv_ready")
        ln_var_step = sem("ln_var_step")
        ln_rstd_ready = sem("ln_rstd_ready")
        xln_ready = sem("xln_ready")
        agg_done = sem("agg_done")
        agg_copied = sem("agg_copied")
        h1_done = sem("h1_done")
        h1_ready = sem("h1_ready")
        h1_counted = sem("h1_counted")
        bn_mv_ready = sem("bn_mv_ready")
        bn_var_step = sem("bn_var_step")
        bn_rstd_ready = sem("bn_rstd_ready")
        bn_step = sem("bn_step")
        bn_ready = sem("bn_ready")
        relu_done = sem("relu_done")
        y_done = sem("y_done")
        y_ready = sem("y_ready")
        y_counted = sem("y_counted")
        y_normed = sem("y_normed")
        y_turned = sem("y_turned")
        x2_ready = sem("x2_ready")
        x_normed = sem("x_normed")
        xt_done = sem("xt_done")
        xt_hi_ready = sem("xt_hi_ready")
        xt_lo_ready = sem("xt_lo_ready")
        gate_done = sem("gate_done")
        gate_step = sem("gate_step")
        mask_ready = sem("mask_ready")
        mask_turned = sem("mask_turned")
        mask_t_ready = sem("mask_t_ready")
        mask_stored = sem("mask_stored")
        mask_loaded = [sem(f"mask_loaded{u}") for u in range(2)]
        up_done = sem("up_done")
        gelu_done = sem("gelu_done")
        hi_done = sem("hi_done")
        lo_done = sem("lo_done")
        down_done = sem("down_done")
        masked = sem("masked")
        added = sem("added")
        sum_turned = sem("sum_turned")
        out_ready = sem("out_ready")
        out_stored = [sem(f"out_stored{u}") for u in range(2)]

        block = ctx.enter_context(nc.Block())

        def group_tiles(g):
            return x_sb[:, bass.ds(g * J, J), :]

        def group_columns(buf, g):
            return buf[:, bass.ds(g * T, T)]

        @block.sync
        def _(sp):
            wait_count = ctx.enter_context(sp.register("wait_count"))
            sp.dma_start(adj_sb[:], adj.rearrange("(p k) m -> p k m", k=KT)).then_inc(adj_loaded, 16)
            per = B // LOADS

            def load_x(i):
                sp.dma_start(x_sb[:, i * per * KT:(i + 1) * per * KT, :].rearrange("p (b k) d -> p b (k d)", k=KT),
                             x_rows[:, i * per:(i + 1) * per, :]).then_inc(x_load[i], 16)

            load_x(0)
            sp.wait_ge(vec_zeroed, 1)
            for name, source in (("gb1", gb1), ("gg1", gg1), ("gbe1", gbe1), ("gb2", gb2), ("gg2", gg2), ("gbe2", gbe2)):
                rows = source.shape[0] // P
                sp.dma_start(vec_rows[names[name]:names[name] + rows, :],
                             source.rearrange("(k p) -> k p", p=P)).then_inc(vec_loaded, 16)
            sp.dma_start(vec_rows[names["fb1"]:names["fb1"] + E * FT, :],
                         fb1.rearrange("e (f p) -> (e f) p", p=P)).then_inc(vec_loaded, 16)
            sp.dma_start(vec_rows[names["fb2"]:names["fb2"] + E, :], fb2).then_inc(vec_loaded, 16)
            sp.dma_start(gw1_raw[:], gw1.rearrange("(k p) d -> p k d", p=P)).then_inc(gw_loaded, 16)
            sp.dma_start(gw2_raw[:], gw2).then_inc(gw_loaded, 16)
            for i in range(1, LOADS):
                load_x(i)
            sp.dma_start(wg_raw[:], wg).then_inc(fw_loaded, 16)
            sp.dma_start(bg_sb[:], bg.unsqueeze(0).to_broadcast([P, E])).then_inc(fw_loaded, 16)
            sp.dma_start(fw_raw[:, 0:W1C].rearrange("p (e h) -> p e h", e=E),
                         fw1.rearrange("e d h -> d e h")).then_inc(fw_loaded, 16)
            sp.dma_start(fw_raw[:, W1C:W1C + W2C].rearrange("p (e f d) -> p e f d", e=E, f=FT),
                         fw2.rearrange("e (f p) d -> p e f d", p=P)).then_inc(fw_loaded, 16)
            for i in range(LOADS):
                sp.wait_ge(x_load[i], 16)
                sp.sem_inc(x_loaded, G // LOADS)

            def spread_mask(g, i, u):
                sp.wait_ge(mask_t_ready, g + 1)
                sp.dma_start(mask_dram[u], mask_t[:]).then_inc(mask_stored, 16)
                settled = held(sp, wait_count, g * 16 + 16)
                sp.wait_ge(vec_zeroed, 1)
                sp.wait_ge(mask_stored, settled)
                sp.wait_ge(masked, from_zero((g - 1) * E))
                sp.dma_start(mask_bc[:, u].rearrange("p e t -> p (e t)"),
                             mask_dram[u].rearrange("r q -> (r q)").unsqueeze(0).to_broadcast([P, E * T])
                             ).then_inc(mask_loaded[u], 16)

            def store_out(g, u):
                settled = held(sp, wait_count, g + 1)
                sp.wait_ge(vec_zeroed, 1)
                sp.wait_ge(out_ready, settled)
                sp.dma_start(out_rows[:, bass.ds(g * BG, BG), :],
                             out_sb[:, u].rearrange("p (b k) d -> p b (k d)", k=KT)).then_inc(out_stored[u], 16)

            sp.wait_ge(fw_split, 4)
            spread_mask(0, 0, 0)

            def turn(i, first=False, last=False):
                for u in range(2):
                    g = i * 2 + u
                    if not (first and u == 0):
                        store_out(g - 1, 1 - u)
                    if not (last and u == 1):
                        spread_mask(g + 1, i, 1 - u)

            turn(0, first=True)
            with sp.Fori(1, PAIRS - 1) as i:
                turn(i)
            turn(PAIRS - 1, last=True)
            store_out(G - 1, 1)
            for u in range(2):
                sp.wait_ge(out_stored[u], PAIRS * 16)

        @block.gpsimd
        def _(pool):
            wait_count = ctx.enter_context(pool.register("wait_count"))
            steps = 0

            def const(ins):
                nonlocal steps
                steps += 1
                ins.then_inc(const_ready, 1)

            pool.memset(vec_rows[:], 0.0).then_inc(vec_zeroed, 1)
            const(pool.memset(eye[:], 0.0))
            const(pool.memset(ident[:], 0.0))
            pool.wait_ge(const_ready, steps)
            for k in range(KT):
                const(pool.affine_select(out=eye[:, k, :], in_=eye[:, k, :], compare_op=ALU.not_equal, fill=1.0,
                                         base=k, pattern=[[-1, N]], channel_multiplier=KT))
            const(pool.affine_select(out=ident[:], in_=ident[:], compare_op=ALU.not_equal, fill=1.0,
                                     base=0, pattern=[[-1, P]], channel_multiplier=1))
            const(pool.memset(ones[:], 1.0))
            const(pool.memset(minus_half[:], -0.5))
            for e in range(E):
                const(pool.memset(expert_number[:, :, e], float(e)))
            pool.wait_ge(const_ready, steps)
            const(pool.tensor_copy(ident_bf[:], ident[:]))
            pool.wait_ge(const_ready, steps)
            pool.wait_ge(deg_ready, 1)
            pool.tensor_tensor(dinv[:], deg[:], minus_half[:, 0:KT], ALU.pow).then_inc(dinv_ready, 1)

            def layer_norm_rstd(n, u):
                settled = held(pool, wait_count, n + 1)
                pool.wait_ge(vec_zeroed, 1)
                pool.wait_ge(ln_mv_ready, settled)
                pool.tensor_scalar(x_var[:, u], x_mv[:, u, :, 1], EPS, None, ALU.add).then_inc(ln_var_step, 1)
                pool.wait_ge(ln_var_step, n + 1)
                pool.tensor_tensor(x_rstd[:, u], x_var[:, u], minus_half[:], ALU.pow).then_inc(ln_rstd_ready, 1)

            def batch_norm_rstd(at, mean_var, count, done):
                pool.wait_ge(bn_mv_ready, done)
                pool.tensor_scalar(bn_var[:, at:at + count], mean_var, EPS, None, ALU.add).then_inc(bn_var_step, 1)
                pool.wait_ge(bn_var_step, done)
                pool.tensor_tensor(bn_rstd[:, at:at + count], bn_var[:, at:at + count], minus_half[:, 0:count],
                                   ALU.pow).then_inc(bn_rstd_ready, 1)

            with pool.Fori(0, PAIRS) as i:
                for u in range(2):
                    layer_norm_rstd(i * 2 + u, u)

            batch_norm_rstd(0, h_mv[:, :, 1], HT, 1)
            pool.wait_ge(fw_loaded, 64)
            for a, b in ((0, W1C), (W1C, W1C + W2C)):
                pool.tensor_copy(fw_hi[:, a:b], fw_raw[:, a:b]).then_inc(fw_split, 1)
            pool.wait_ge(fw_split, 2)
            for a, b in ((0, W1C), (W1C, W1C + W2C)):
                pool.tensor_tensor(fw_lo[:, a:b], fw_raw[:, a:b], fw_hi[:, a:b].bitcast(F32),
                                   ALU.subtract).then_inc(fw_split, 1)
            batch_norm_rstd(HT, y_mv[:, 1:2], 1, 2)

            layer_norm_rstd(G, 0)

            def turn(i, last=False):
                for u in range(2):
                    g = i * 2 + u
                    for e in range(E):
                        if e == 2 and not (last and u == 1):
                            layer_norm_rstd(g + 1 + G, 1 - u)
                        if e >= 1:
                            pool.wait_ge(masked, g * E + e + 1)
                            pool.wait_ge(added, from_zero(g * (E - 1) + e - 1))
                            pool.tensor_tensor(ffn_sum[:, u], ffn_sum[:, u], y_masked[:, e % 2],
                                               ALU.add).then_inc(added, 1)

            turn(0)
            with pool.Fori(1, PAIRS - 1) as i:
                turn(i)
            turn(PAIRS - 1, last=True)

        @block.scalar
        def _(act):
            def evacuate_hidden(g, u):
                act.wait_ge(h1_done, g + 1)
                for k in range(HT):
                    act.activation(group_columns(h1[:, k, :], g), h1_ps[:, u, k, :], ACT.Identity,
                                   bias=column("gb1", k)).then_inc(h1_ready, 1)

            def evacuate_aggregate(g, u):
                act.wait_ge(agg_done, g + 1)
                act.copy(agg_t[:, u], agg_ps[:, u]).then_inc(agg_copied, 1)

            act.wait_ge(weights_ready, 2)
            evacuate_aggregate(0, 0)
            evacuate_aggregate(1, 1)
            evacuate_hidden(0, 0)
            with act.Fori(0, PAIRS - 1) as i:
                for u in range(2):
                    evacuate_aggregate(i * 2 + 2 + u, u)
                    evacuate_hidden(i * 2 + 1 + u, 1 - u)
            evacuate_hidden(G - 1, 1)

            act.wait_ge(bn_ready, 1)

            def relu(i):
                for u in range(2):
                    g = i * 2 + u
                    act.wait_ge(y_done, from_zero(g - 1))
                    for k in range(HT):
                        act.activation(h_relu[:, u, k, :], group_columns(h1[:, k, :], g), ACT.Relu,
                                       bias=bn_shift[:, k:k + 1], scale=bn_scale[:, k:k + 1]).then_inc(relu_done, 1)

            relu(0)
            with act.Fori(1, PAIRS) as i:
                relu(i)

            def split_hi_x(n, u):
                act.wait_ge(xt_done, n + 1)
                act.copy(xt_hi[:, u], work_b).then_inc(xt_hi_ready, 1)

            split_hi_x(0, 0)

            def turn(i, last=False):
                for u in range(2):
                    g = i * 2 + u
                    for e in range(E):
                        q = g * E + e
                        r = e % 2
                        for f in range(FT):
                            act.wait_ge(up_done, q * FT + f + 1)
                            if f == 0:
                                act.wait_ge(lo_done, from_zero(q - 1))
                            act.activation(hid[:, r, f, :], hid_ps[:, r, f, :], ACT.Gelu,
                                           bias=column("fb1", e * FT + f)).then_inc(gelu_done, 1)
                        act.wait_ge(gelu_done, (q + 1) * FT)
                        act.wait_ge(down_done, from_zero(q - 1))
                        act.copy(hid_hi[:, r], hid[:, r]).then_inc(hi_done, 1)
                        if e == 4 and not (last and u == 1):
                            split_hi_x(g + 1, 1 - u)

            turn(0)
            with act.Fori(1, PAIRS - 1) as i:
                turn(i)
            turn(PAIRS - 1, last=True)

        @block.vector
        def _(dve):
            wait_count = ctx.enter_context(dve.register("wait_count"))
            dve.wait_ge(const_ready, 5)
            dve.wait_ge(adj_loaded, 16)
            dve.tensor_tensor(adj_sb[:], adj_sb[:], eye[:], ALU.add).then_inc(adj_step, 1)
            dve.wait_ge(adj_step, 1)
            dve.tensor_reduce(row_sum[:], adj_sb[:], AX_X, ALU.add).then_inc(adj_step, 1)
            dve.tensor_tensor(eye_adj[:], adj_sb[:], eye[:], ALU.mult).then_inc(adj_step, 1)
            dve.wait_ge(adj_step, 3)
            dve.tensor_reduce(diag[:], eye_adj[:], AX_X, ALU.add).then_inc(adj_step, 1)
            dve.wait_ge(col_sum_done, 1)
            dve.tensor_tensor(deg[:], work_a[:, 0:KT], row_sum[:], ALU.add).then_inc(adj_step, 1)
            dve.wait_ge(adj_step, 5)
            dve.tensor_tensor(deg[:], deg[:], diag[:], ALU.subtract).then_inc(deg_ready, 1)
            dve.wait_ge(weights_turned, 1)
            dve.tensor_copy(vec[:], h1_ps[:, 0, 0, 0:P]).then_inc(weights_ready, 1)
            dve.wait_ge(weights_turned, 2)
            dve.tensor_copy(gw_t[:], h1_ps[:, 0, 1, :].rearrange("p (c q) -> p c q", q=P)).then_inc(weights_ready, 1)

            def layer_norm_stats(g, n, u):
                tiles = group_tiles(g)
                for j in range(J):
                    ins = dve.bn_stats(x_stats[:, u, j, :], tiles[:, j, :])
                ins.then_inc(ln_stats_step, 1)
                settled = held(dve, wait_count, n + 1)
                dve.wait_ge(vec_zeroed, 1)
                dve.wait_ge(ln_stats_step, settled)
                for j in range(J):
                    ins = dve.bn_aggr(x_mv[:, u, j, :], x_stats[:, u, j, :])
                ins.then_inc(ln_mv_ready, 1)

            def layer_norm_apply(target, g, n, u, ready):
                dve.wait_ge(ln_rstd_ready, n + 1)
                tiles = group_tiles(g)
                for j in range(J):
                    ins = dve.tensor_scalar(target[:, j, :], tiles[:, j, :], x_mv[:, u, j, 0:1],
                                            x_rstd[:, u, j:j + 1], ALU.subtract, ALU.mult)
                ins.then_inc(ready, 1)

            def hidden_stats(g):
                settled = held(dve, wait_count, g * HT + HT)
                dve.wait_ge(vec_zeroed, 1)
                dve.wait_ge(h1_ready, settled)
                for k in range(HT):
                    ins = dve.bn_stats(h_stats[:, k, bass.ds(g, 1), :].rearrange("p a s -> p (a s)"),
                                       group_columns(h1[:, k, :], g))
                ins.then_inc(h1_counted, 1)

            dve.wait_ge(x_loaded, 1)
            layer_norm_stats(0, 0, 0)
            dve.wait_ge(dinv_ready, 1)
            for k in range(KT):
                dve.tensor_scalar(adj_sb[:, k, :], adj_sb[:, k, :], dinv[:, k:k + 1], None,
                                  ALU.mult).then_inc(adj_scaled, 1)
            dve.wait_ge(adj_turned, 1)
            for k in range(KT):
                dve.tensor_scalar(a_t[:, k, :], work_b[:, k * N:(k + 1) * N], dinv[:, k:k + 1], None,
                                  ALU.mult).then_inc(a_t_ready, 1)

            def gnn_turn(i, first=False, last=False):
                for u in range(2):
                    g = i * 2 + u
                    if not (last and u == 1):
                        settled = held(dve, wait_count, g + 2)
                        dve.wait_ge(vec_zeroed, 1)
                        dve.wait_ge(x_loaded, settled)
                        layer_norm_stats(g + 1, g + 1, 1 - u)
                    dve.wait_ge(agg_done, from_zero(g - 1))
                    layer_norm_apply(xln[:, u], g, g, u, xln_ready)
                    if not (first and u == 0):
                        hidden_stats(g - 1)

            gnn_turn(0, first=True)
            with dve.Fori(1, PAIRS - 1) as i:
                gnn_turn(i)
            gnn_turn(PAIRS - 1, last=True)
            hidden_stats(G - 1)

            def batch_norm(at, count, mean, gamma, beta, done):
                dve.wait_ge(bn_rstd_ready, done)
                c = slice(at, at + count)
                dve.tensor_tensor(bn_scale[:, c], bn_rstd[:, c], gamma, ALU.mult).then_inc(bn_step, 1)
                dve.wait_ge(bn_step, from_zero(2 * done - 1))
                dve.tensor_tensor(bn_mean_scaled[:, c], mean, bn_scale[:, c], ALU.mult).then_inc(bn_step, 1)
                dve.wait_ge(bn_step, 2 * done)
                dve.tensor_tensor(bn_shift[:, c], beta, bn_mean_scaled[:, c], ALU.subtract).then_inc(bn_ready, 1)

            dve.wait_ge(h1_counted, G)
            for k in range(HT):
                ins = dve.bn_aggr(h_mv[:, k, :], h_stats[:, k].rearrange("p g s -> p (g s)"))
            ins.then_inc(bn_mv_ready, 1)
            batch_norm(0, HT, h_mv[:, :, 0], vec[:, names["gg1"]:names["gg1"] + HT],
                       vec[:, names["gbe1"]:names["gbe1"] + HT], 1)
            dve.wait_ge(fw_loaded, 64)
            dve.tensor_copy(wg_hi[:], wg_raw[:]).then_inc(wg_split, 1)
            dve.wait_ge(wg_split, 1)
            dve.tensor_tensor(wg_lo[:], wg_raw[:], wg_hi[:].bitcast(F32), ALU.subtract).then_inc(wg_split, 1)

            with dve.Fori(0, PAIRS) as i:
                for u in range(2):
                    g = i * 2 + u
                    dve.wait_ge(y_done, g + 1)
                    dve.tensor_scalar(group_columns(y, g), y_ps[:, u], column("gb2"), None,
                                      ALU.add).then_inc(y_ready, 1)
                    settled = held(dve, wait_count, g + 1)
                    dve.wait_ge(vec_zeroed, 1)
                    dve.wait_ge(y_ready, settled)
                    dve.bn_stats(y_stats[:, bass.ds(g, 1), :].rearrange("p a s -> p (a s)"),
                                 group_columns(y, g)).then_inc(y_counted, 1)
            dve.wait_ge(y_counted, G)
            dve.bn_aggr(y_mv[:], y_stats[:].rearrange("p g s -> p (g s)")).then_inc(bn_mv_ready, 1)
            batch_norm(HT, 1, y_mv[:, 0:1], column("gg2"), column("gbe2"), 2)
            dve.wait_ge(bn_ready, 2)

            def norm_y(n):
                dve.wait_ge(y_turned, from_zero(n))
                dve.tensor_scalar(y_norm, group_columns(y, n), bn_scale[:, HT:HT + 1], bn_shift[:, HT:HT + 1],
                                  ALU.mult, ALU.add).then_inc(y_normed, 1)

            def add_residual(n, u):
                dve.wait_ge(y_turned, n + 1)
                tiles = group_tiles(n)
                dve.tensor_tensor(tiles, work_a.rearrange("p (j d) -> p j d", j=J), tiles, ALU.add).then_inc(x2_ready, 1)
                settled = held(dve, wait_count, n + 1)
                dve.wait_ge(vec_zeroed, 1)
                dve.wait_ge(x2_ready, settled)
                layer_norm_stats(n, n + G, u)

            def norm_x(n, u):
                dve.wait_ge(xt_done, from_zero(n))
                layer_norm_apply(x_norm, n, n + G, u, x_normed)

            def split_lo_x(n, u):
                dve.wait_ge(xt_hi_ready, n + 1)
                dve.tensor_tensor(xt_lo[:, u], work_b, xt_hi[:, u].bitcast(F32), ALU.subtract).then_inc(xt_lo_ready, 1)

            def pick_experts(n):
                dve.wait_ge(gate_done, n + 1)
                bias = bg_sb[:].unsqueeze(1).to_broadcast([P, J, E])
                dve.tensor_tensor(gate[:], work_a[:, 0:J * E].rearrange("p (j e) -> p j e", j=J), bias,
                                  ALU.add).then_inc(gate_step, 1)
                settled = held(dve, wait_count, n * 4 + 1)
                dve.wait_ge(vec_zeroed, 1)
                dve.wait_ge(gate_step, settled)
                for j in range(J):
                    ins = dve.max(gate_max[:, j, :], gate[:, j, :])
                ins.then_inc(gate_step, 1)
                settled = held(dve, wait_count, n * 4 + 2)
                dve.wait_ge(vec_zeroed, 1)
                dve.wait_ge(gate_step, settled)
                for j in range(J):
                    ins = dve.max_index(gate_idx[:, j, :], gate_max[:, j, :], gate[:, j, :])
                ins.then_inc(gate_step, 1)
                dve.wait_ge(gate_step, n * 4 + 3)
                for k in range(2):
                    ins = dve.tensor_tensor(picked[:, k], expert_number[:],
                                            gate_idx[:, :, k:k + 1].to_broadcast([P, J, E]), ALU.is_equal)
                ins.then_inc(gate_step, 1)
                dve.wait_ge(gate_step, n * 4 + 4)
                dve.wait_ge(mask_turned, from_zero(n))
                dve.tensor_tensor(mask[:].rearrange("p e j -> p j e"), picked[:, 0], picked[:, 1],
                                  ALU.add).then_inc(mask_ready, 1)

            def copy_mask(n):
                dve.wait_ge(mask_turned, n + 1)
                dve.wait_ge(mask_stored, from_zero(n * 16))
                dve.tensor_copy(mask_t[:], work_b[0:E * J, 0:P]).then_inc(mask_t_ready, 1)

            def mask_expert(g, e, i, u):
                q = g * E + e
                dve.wait_ge(down_done, q + 1)
                if e == 0:
                    dve.wait_ge(mask_loaded[u], i * 16 + 16)
                    dve.wait_ge(sum_turned, from_zero(g - 1))
                    target = ffn_sum[:, u]
                else:
                    dve.wait_ge(added, from_zero(g * (E - 1) + (e - 2 if e > 2 else 0)))
                    target = y_masked[:, e % 2]
                dve.scalar_tensor_tensor(out=target, in0=ffn_ps[:, e % 2], scalar=column("fb2", e),
                                         in1=mask_bc[:, u, e, :], op0=ALU.add, op1=ALU.mult).then_inc(masked, 1)

            def split_lo_hidden(g, e):
                q = g * E + e
                dve.wait_ge(hi_done, q + 1)
                dve.wait_ge(down_done, from_zero(q - 1))
                dve.tensor_tensor(hid_lo[:, e % 2], hid[:, e % 2], hid_hi[:, e % 2].bitcast(F32),
                                  ALU.subtract).then_inc(lo_done, 1)

            def finish(o, i, u):
                dve.wait_ge(sum_turned, o + 1)
                dve.wait_ge(out_stored[u], from_zero(i * 16))
                dve.tensor_tensor(out_sb[:, u], work_b.rearrange("p (j d) -> p j d", j=J), group_tiles(o),
                                  ALU.add).then_inc(out_ready, 1)

            norm_y(0)
            add_residual(0, 0)
            norm_x(0, 0)
            split_lo_x(0, 0)
            pick_experts(0)
            copy_mask(0)

            def turn(i, first=False, last=False):
                for u in range(2):
                    g = i * 2 + u
                    prepare = not (last and u == 1)
                    for e in range(E):
                        q = g * E + e
                        if e >= 2:
                            mask_expert(g, e - 2, i, u)
                        elif not (first and u == 0):
                            mask_expert(g - 1, E - 2 + e, i, 1 - u)
                        if prepare:
                            if e == 0:
                                norm_y(g + 1)
                            if e == 1:
                                add_residual(g + 1, 1 - u)
                            if e == 3:
                                norm_x(g + 1, 1 - u)
                            if e == 4:
                                split_lo_x(g + 1, 1 - u)
                            if e == 6:
                                pick_experts(g + 1)
                            if e == 7:
                                copy_mask(g + 1)
                        if e == 5 and not (first and u == 0):
                            finish(g - 1, i if u else i - 1, 1 - u)
                        split_lo_hidden(g, e)

            turn(0, first=True)
            with dve.Fori(1, PAIRS - 1) as i:
                turn(i)
            turn(PAIRS - 1, last=True)
            for e in (E - 2, E - 1):
                mask_expert(G - 1, e, PAIRS - 1, 1)
            finish(G - 1, PAIRS - 1, 1)

        @block.tensor
        def _(pe):
            def turn_tiles(target, source, count):
                for j in range(count):
                    ins = pe.transpose(target[:, j * P:(j + 1) * P], source(j), ident[:])
                return ins

            pe.wait_ge(const_ready, 16)
            pe.wait_ge(adj_step, 1)
            for k in range(KT):
                for l in range(KT):
                    ins = pe.matmul(work_a[:, k:k + 1], adj_sb[:, l, k::KT], ones[:, 0:1],
                                    start=(l == 0), stop=(l == KT - 1))
            ins.then_inc(col_sum_done, 1)
            pe.wait_ge(vec_loaded, 8 * 16)
            pe.transpose(h1_ps[:, 0, 0, 0:P], vec_rows[:], ident[:]).then_inc(weights_turned, 1)
            pe.wait_ge(gw_loaded, 32)
            ins = turn_tiles(h1_ps[:, 0, 1, :],
                             lambda c: gw1_raw[:, c, :] if c < HT else gw2_raw[:, (c - HT) * P:(c - HT + 1) * P], 2 * HT)
            ins.then_inc(weights_turned, 1)
            pe.wait_ge(adj_scaled, KT)
            ins = turn_tiles(work_b, lambda c: adj_sb[:, c % KT, (c // KT)::KT], KT * KT)
            ins.then_inc(adj_turned, 1)
            pe.wait_ge(a_t_ready, KT)
            pe.wait_ge(weights_ready, 2)

            def aggregate(g, u):
                pe.wait_ge(xln_ready, g + 1)
                pe.wait_ge(agg_copied, from_zero(g - 1))
                for b in range(BG):
                    for k in range(KT):
                        ins = pe.matmul(agg_ps[:, u, b * N:(b + 1) * N], xln[:, u, b * KT + k, :], a_t[:, k, :],
                                        start=(k == 0), stop=(k == KT - 1))
                ins.then_inc(agg_done, 1)

            def hidden(g, u):
                pe.wait_ge(agg_copied, g + 1)
                pe.wait_ge(h1_ready, from_zero((g - 1) * HT))
                for k in range(HT):
                    ins = pe.matmul(h1_ps[:, u, k, :], gw_t[:, k, :], agg_t[:, u], start=True, stop=True)
                ins.then_inc(h1_done, 1)

            aggregate(0, 0)
            aggregate(1, 1)
            hidden(0, 0)
            aggregate(2, 0)
            hidden(1, 1)
            with pe.Fori(1, PAIRS - 1) as i:
                for u in range(2):
                    aggregate(i * 2 + 1 + u, 1 - u)
                    hidden(i * 2 + u, u)
            aggregate(G - 1, 1)
            hidden(G - 2, 0)
            hidden(G - 1, 1)

            def second_layer(i):
                for u in range(2):
                    g = i * 2 + u
                    pe.wait_ge(relu_done, g * HT + HT)
                    pe.wait_ge(y_ready, from_zero(g - 1))
                    for k in range(HT):
                        ins = pe.matmul(y_ps[:, u], gw_t[:, HT + k, :], h_relu[:, u, k, :],
                                        start=(k == 0), stop=(k == HT - 1))
                    ins.then_inc(y_done, 1)

            second_layer(0)
            with pe.Fori(1, PAIRS) as i:
                second_layer(i)

            def turn_y(n):
                pe.wait_ge(y_normed, n + 1)
                pe.wait_ge(gate_step, from_zero((n - 1) * 4 + 1))
                turn_tiles(work_a, lambda j: y_norm[:, j * P:(j + 1) * P], J).then_inc(y_turned, 1)

            def turn_x(n):
                pe.wait_ge(x_normed, n + 1)
                pe.wait_ge(mask_t_ready, from_zero(n))
                turn_tiles(work_b, lambda j: x_norm[:, j, :], J).then_inc(xt_done, 1)

            def gate_scores(n, u):
                pe.wait_ge(xt_lo_ready, n + 1)
                pe.wait_ge(x2_ready, n + 1)
                for j in range(J):
                    c = slice(j * P, (j + 1) * P)
                    o = work_a[:, j * E:(j + 1) * E]
                    pe.matmul(o, xt_hi[:, u, c], wg_hi[:], start=True, stop=False)
                    pe.matmul(o, xt_hi[:, u, c], wg_lo[:], start=False, stop=False)
                    ins = pe.matmul(o, xt_lo[:, u, c], wg_hi[:], start=False, stop=True)
                ins.then_inc(gate_done, 1)

            def turn_mask(n):
                pe.wait_ge(mask_ready, n + 1)
                pe.wait_ge(out_ready, from_zero(n - 1))
                pe.matmul(work_b[0:E * J, 0:P], mask[:].rearrange("p e j -> p (e j)"), ident_bf[:],
                          start=True, stop=True).then_inc(mask_turned, 1)

            def turn_sum(o, u, last=False):
                pe.wait_ge(added, (o + 1) * (E - 1))
                pe.wait_ge(xt_lo_ready, G if last else o + 2)
                turn_tiles(work_b, lambda j: ffn_sum[:, u, j * P:(j + 1) * P], J).then_inc(sum_turned, 1)

            def up(g, e, u):
                q = g * E + e
                if e == 0:
                    pe.wait_ge(xt_lo_ready, g + 1)
                pe.wait_ge(gelu_done, from_zero((q - 1) * FT))
                for f in range(FT):
                    o = hid_ps[:, e % 2, f, :]
                    pe.matmul(o, w1(fw_hi, e, f), xt_hi[:, u], start=True, stop=False)
                    pe.matmul(o, w1(fw_hi, e, f), xt_lo[:, u], start=False, stop=False)
                    pe.matmul(o, w1(fw_lo, e, f), xt_hi[:, u], start=False, stop=True).then_inc(up_done, 1)

            def down(g, e):
                q = g * E + e
                pe.wait_ge(lo_done, q + 1)
                pe.wait_ge(masked, from_zero(q - 1))
                o = ffn_ps[:, e % 2]
                for f in range(FT):
                    pe.matmul(o, w2(fw_hi, e, f), hid_hi[:, e % 2, f, :], start=(f == 0), stop=False)
                    pe.matmul(o, w2(fw_hi, e, f), hid_lo[:, e % 2, f, :], start=False, stop=False)
                    ins = pe.matmul(o, w2(fw_lo, e, f), hid_hi[:, e % 2, f, :], start=False, stop=(f == FT - 1))
                ins.then_inc(down_done, 1)

            turn_y(0)
            turn_x(0)
            pe.wait_ge(wg_split, 2)
            gate_scores(0, 0)
            turn_mask(0)
            pe.wait_ge(fw_split, 4)

            def turn(i, first=False, last=False):
                for u in range(2):
                    g = i * 2 + u
                    prepare = not (last and u == 1)
                    for e in range(E):
                        up(g, e, u)
                        if prepare:
                            if e == 1:
                                turn_y(g + 1)
                            if e == 4:
                                turn_x(g + 1)
                            if e == 5:
                                gate_scores(g + 1, 1 - u)
                        if e == 5 and not (first and u == 0):
                            turn_sum(g - 1, 1 - u)
                        if e == 7 and prepare:
                            turn_mask(g + 1)
                        if e >= 2:
                            down(g, e - 2)
                        elif not (first and u == 0):
                            down(g - 1, E - 2 + e)

            turn(0, first=True)
            with pe.Fori(1, PAIRS - 1) as i:
                turn(i)
            turn(PAIRS - 1, last=True)
            for e in (E - 2, E - 1):
                down(G - 1, e)
            turn_sum(G - 1, 1, last=True)


_INS = ["x", "adj", "L0_gnn_W1", "L0_gnn_b1", "L0_gnn_g1", "L0_gnn_be1", "L0_gnn_W2", "L0_gnn_b2", "L0_gnn_g2",
        "L0_gnn_be2", "L0_ffn_Wg", "L0_ffn_bg", "L0_ffn_W1", "L0_ffn_b1", "L0_ffn_W2", "L0_ffn_b2"]


def kernel(**inputs):
    import numpy as _np
    import concourse.bacc as _bacc
    from concourse import mybir as _mybir
    from concourse.bass_utils import run_bass_kernel_spmd as _run

    nc = _bacc.Bacc("TRN2", target_bir_lowering=False, num_devices=1)
    arrays, args = {}, []
    for name in _INS:
        a = _np.ascontiguousarray(inputs[name])
        arrays[f"in_{name}_dram"] = a
        args.append(nc.dram_tensor(f"in_{name}_dram", a.shape, _mybir.dt.from_np(a.dtype), kind="ExternalInput").ap())
    shape = inputs["x"].shape
    out = nc.dram_tensor("out_0_dram", shape, _mybir.dt.float32, kind="ExternalOutput").ap()
    gnn_moe_program(nc, *args, out)
    r = _run(nc, [arrays], core_ids=[0])
    return r.results[0]["out_0_dram"]
```

```python
from contextlib import ExitStack

import concourse.bass as bass
from concourse import mybir

F32 = mybir.dt.float32
F32R = mybir.dt.float32r
BF16 = mybir.dt.bfloat16
U32 = mybir.dt.uint32
ALU = mybir.AluOpType
ACT = mybir.ActivationFunctionType
AX_X = mybir.AxisListType.X

P = 128
EPS = 1e-5


def from_zero(value):
    return max(value, 0) if isinstance(value, int) else value


def held(engine, register, value):
    if isinstance(value, int):
        return value
    engine.reg_mov(register, value)
    return register


def gnn_moe_program(nc, x, adj, gw1, gb1, gg1, gbe1, gw2, gb2, gg2, gbe2, wg, bg, fw1, fb1, fw2, fb2, out):
    B, N, D = x.shape
    H = gw1.shape[0]
    E, _, FH = fw1.shape
    KT = N // P
    HT = H // P
    FT = FH // P
    BG = 2
    G = B // BG
    T = BG * N
    J = T // P
    PAIRS = G // 2
    LOADS = 8
    LAG = 3
    RING = 4
    PICK_STEPS = 5
    assert D == P and KT == 2 and HT == 2 and FT == 2 and T == 512 and G % LOADS == 0

    x_rows = x.rearrange("b (p k) d -> p b (k d)", k=KT)
    out_rows = out.rearrange("b (p k) d -> p b (k d)", k=KT)

    with ExitStack() as ctx:
        def sb(name, shape, dt):
            return ctx.enter_context(nc.sbuf_tensor(name, shape, dt))

        def sem(name):
            return ctx.enter_context(nc.semaphore(name))

        x_sb = sb("x_sb", [P, G * J, D], F32)
        h1 = sb("h1", [P, HT, G * T], F32)
        y = h1[:, 0, :]
        spare = h1[:, 1, :]
        ident = sb("ident", [P, P], F32)
        ident_bf = sb("ident_bf", [P, P], BF16)
        ones = sb("ones", [P, 2], F32)
        minus_half = sb("minus_half", [P, J], F32)
        expert_number = sb("expert_number", [P, J, E], F32)
        zero_col = sb("zero_col", [P, 1], F32)

        adj_sb = sb("adj_sb", [P, KT, N], F32)
        eye = sb("eye", [P, KT, N], F32)
        eye_adj = h1[:, 1, 0:KT * N].rearrange("p (k m) -> p k m", k=KT)
        a_t = sb("a_t", [P, KT, N], F32)
        row_sum = sb("row_sum", [P, KT], F32)
        diag = sb("diag", [P, KT], F32)
        deg = sb("deg", [P, KT], F32)
        dinv = sb("dinv", [P, KT], F32)

        NV = 3 * HT + 3 + E * FT + E
        vec_rows = sb("vec_rows", [P, P], F32)
        vec = sb("vec", [P, P], F32)
        names, at = {}, 0
        for name, rows in (("gb1", HT), ("gg1", HT), ("gbe1", HT), ("gb2", 1), ("gg2", 1), ("gbe2", 1),
                            ("fb1", E * FT), ("fb2", E)):
            names[name] = at
            at += rows
        assert at == NV

        def column(name, k=0):
            return vec[:, names[name] + k:names[name] + k + 1]

        gw1_raw = sb("gw1_raw", [P, HT, D], F32)
        gw2_raw = sb("gw2_raw", [P, H], F32)
        gw_t = sb("gw_t", [P, 2 * HT, P], F32)
        bg_sb = sb("bg_sb", [P, E], F32)
        wg_raw = sb("wg_raw", [P, E], F32)
        wg_parts = sb("wg_parts", [P, 2, E], F32R)

        W1C = E * FH
        W2C = E * FT * D
        fw_raw = sb("fw_raw", [P, W1C + W2C], F32)
        fw_hi = sb("fw_hi", [P, W1C + W2C], F32R)
        fw_lo = sb("fw_lo", [P, W1C + W2C], F32R)
        mask_bc = fw_raw[:].bitcast(BF16)[:, 0:2 * E * T].rearrange("p (u e t) -> p u e t", u=2, e=E)

        def w1(part, e, f):
            return part[:, e * FH + f * P:e * FH + (f + 1) * P]

        def w2(part, e, f):
            at = W1C + (e * FT + f) * D
            return part[:, at:at + D]

        phase_buf = sb("phase_buf", [P, 4 * T], F32)
        xln = phase_buf[:, 0:2 * T].rearrange("p (u j d) -> p u j d", u=2, j=J)
        agg_t = phase_buf[:, 2 * T:4 * T].rearrange("p (u t) -> p u t", u=2)
        h_relu = phase_buf[:, :].rearrange("p (u k t) -> p u k t", u=2, k=HT)
        x_stats = sb("x_stats", [P, 2, J, 6], F32)
        x_mv = sb("x_mv", [P, 2, J, 2], F32)
        x_var = sb("x_var", [P, 2, J], F32)
        x_rstd = sb("x_rstd", [P, 2, J], F32)
        h_stats = sb("h_stats", [P, HT, G, 6], F32)
        h_mv = sb("h_mv", [P, HT, 2], F32)
        y_stats = sb("y_stats", [P, G, 6], F32)
        y_mv = sb("y_mv", [P, 2], F32)
        bn_var = sb("bn_var", [P, HT + 1], F32)
        bn_rstd = sb("bn_rstd", [P, HT + 1], F32)
        bn_scale = sb("bn_scale", [P, HT + 1], F32)
        bn_shift = sb("bn_shift", [P, HT + 1], F32)
        bn_mean_scaled = sb("bn_mean_scaled", [P, HT + 1], F32)

        at = 0

        def carve(count):
            nonlocal at
            at += count
            assert at <= G * T
            return spare[:, at - count:at]

        y_norm = carve(T)
        x_norm = carve(T).rearrange("p (j d) -> p j d", j=J)
        hid = carve(RING * FT * T).rearrange("p (r f t) -> p r f t", r=RING, f=FT)
        y_masked = carve(2 * T).rearrange("p (r t) -> p r t", r=2)
        ffn_sum = carve(2 * T).rearrange("p (u t) -> p u t", u=2)
        out_sb = carve(2 * T).rearrange("p (u j d) -> p u j d", u=2, j=J)
        xt_hi = sb("xt_hi", [P, 2, T], F32R)
        xt_lo = sb("xt_lo", [P, 2, T], F32R)
        hid_hi = sb("hid_hi", [P, RING, FT, T], F32R)
        hid_lo = sb("hid_lo", [P, RING, FT, T], F32R)
        gate = sb("gate", [P, J, E], F32)
        gate_max = sb("gate_max", [P, J, 8], F32)
        gate_idx = sb("gate_idx", [P, J, 8], U32)
        picked = sb("picked", [P, 2, J, E], F32)
        mask = sb("mask", [P, E, J], BF16)
        mask_t = sb("mask_t", [E * J, P], BF16)
        mask_dram = nc.dram_tensor("mask_dram", (2, E * J, P), BF16).ap()

        psum = ctx.enter_context(nc.psum_tensor("psum", [P, 8, T], F32))
        agg_ps = psum[:, 0:2, :]
        h1_ps = psum[:, 2:6, :].rearrange("p (u k) t -> p u k t", u=2)
        y_ps = psum[:, 6:8, :]
        hid_ps = psum[:, 0:4, :].rearrange("p (r f) t -> p r f t", r=2)
        ffn_ps = psum[:, 4:6, :]
        work_a = psum[:, 6, :]
        work_b = psum[:, 7, :]

        const_ready = sem("const_ready")
        adj_loaded = sem("adj_loaded")
        vec_zeroed = sem("vec_zeroed")
        vec_loaded = sem("vec_loaded")
        gw_loaded = sem("gw_loaded")
        fw_loaded = sem("fw_loaded")
        x_load = [sem(f"x_load{i}") for i in range(LOADS)]
        x_loaded = sem("x_loaded")
        adj_step = sem("adj_step")
        deg_ready = sem("deg_ready")
        dinv_ready = sem("dinv_ready")
        col_sum_done = sem("col_sum_done")
        adj_scaled = sem("adj_scaled")
        adj_turned = sem("adj_turned")
        a_t_ready = sem("a_t_ready")
        weights_turned = sem("weights_turned")
        weights_ready = sem("weights_ready")
        wg_split = sem("wg_split")
        fw_split = sem("fw_split")
        ln_stats_step = sem("ln_stats_step")
        ln_mv_ready = sem("ln_mv_ready")
        ln_centered = sem("ln_centered")
        ln_var_step = sem("ln_var_step")
        ln_rstd_ready = sem("ln_rstd_ready")
        xln_ready = sem("xln_ready")
        agg_done = sem("agg_done")
        agg_copied = sem("agg_copied")
        h1_done = sem("h1_done")
        h1_ready = sem("h1_ready")
        h1_counted = sem("h1_counted")
        bn_mv_ready = sem("bn_mv_ready")
        bn_var_step = sem("bn_var_step")
        bn_rstd_ready = sem("bn_rstd_ready")
        bn_step = sem("bn_step")
        bn_ready = sem("bn_ready")
        relu_done = sem("relu_done")
        y_done = sem("y_done")
        y_ready = sem("y_ready")
        y_counted = sem("y_counted")
        y_normed = sem("y_normed")
        y_turned = sem("y_turned")
        x2_ready = sem("x2_ready")
        x_normed = sem("x_normed")
        xt_done = sem("xt_done")
        xt_hi_ready = sem("xt_hi_ready")
        xt_lo_ready = sem("xt_lo_ready")
        gate_done = sem("gate_done")
        gate_step = sem("gate_step")
        mask_ready = sem("mask_ready")
        mask_turned = sem("mask_turned")
        mask_t_ready = sem("mask_t_ready")
        mask_stored = sem("mask_stored")
        mask_loaded = [sem(f"mask_loaded{u}") for u in range(2)]
        up_done = sem("up_done")
        gelu_done = sem("gelu_done")
        hi_done = sem("hi_done")
        lo_done = sem("lo_done")
        down_done = sem("down_done")
        masked = sem("masked")
        added = sem("added")
        sum_turned = sem("sum_turned")
        out_ready = sem("out_ready")
        out_stored = [sem(f"out_stored{u}") for u in range(2)]

        block = ctx.enter_context(nc.Block())

        def group_tiles(g):
            return x_sb[:, bass.ds(g * J, J), :]

        def group_columns(buf, g):
            return buf[:, bass.ds(g * T, T)]

        @block.sync
        def _(sp):
            wait_count = ctx.enter_context(sp.register("wait_count"))
            sp.dma_start(adj_sb[:], adj.rearrange("(p k) m -> p k m", k=KT)).then_inc(adj_loaded, 16)
            per = B // LOADS

            def load_x(i):
                sp.dma_start(x_sb[:, i * per * KT:(i + 1) * per * KT, :].rearrange("p (b k) d -> p b (k d)", k=KT),
                             x_rows[:, i * per:(i + 1) * per, :]).then_inc(x_load[i], 16)

            load_x(0)
            sp.dma_start(gw1_raw[:], gw1.rearrange("(k p) d -> p k d", p=P)).then_inc(gw_loaded, 16)
            sp.dma_start(gw2_raw[:], gw2).then_inc(gw_loaded, 16)
            load_x(1)
            sp.wait_ge(vec_zeroed, 1)
            for name, source in (("gb1", gb1), ("gg1", gg1), ("gbe1", gbe1), ("gb2", gb2), ("gg2", gg2), ("gbe2", gbe2)):
                rows = source.shape[0] // P
                sp.dma_start(vec_rows[names[name]:names[name] + rows, :],
                             source.rearrange("(k p) -> k p", p=P)).then_inc(vec_loaded, 16)
            sp.dma_start(vec_rows[names["fb1"]:names["fb1"] + E * FT, :],
                         fb1.rearrange("e (f p) -> (e f) p", p=P)).then_inc(vec_loaded, 16)
            sp.dma_start(vec_rows[names["fb2"]:names["fb2"] + E, :], fb2).then_inc(vec_loaded, 16)
            for i in range(2, LOADS):
                load_x(i)
            sp.dma_start(wg_raw[:], wg).then_inc(fw_loaded, 16)
            sp.dma_start(bg_sb[:], bg.unsqueeze(0).to_broadcast([P, E])).then_inc(fw_loaded, 16)
            sp.dma_start(fw_raw[:, 0:W1C].rearrange("p (e h) -> p e h", e=E),
                         fw1.rearrange("e d h -> d e h")).then_inc(fw_loaded, 16)
            sp.dma_start(fw_raw[:, W1C:W1C + W2C].rearrange("p (e f d) -> p e f d", e=E, f=FT),
                         fw2.rearrange("e (f p) d -> p e f d", p=P)).then_inc(fw_loaded, 16)
            for i in range(LOADS):
                sp.wait_ge(x_load[i], 16)
                sp.sem_inc(x_loaded, G // LOADS)

            def spread_mask(g, i, u):
                sp.wait_ge(mask_t_ready, g + 1)
                sp.dma_start(mask_dram[u], mask_t[:]).then_inc(mask_stored, 16)
                settled = held(sp, wait_count, g * 16 + 16)
                sp.wait_ge(vec_zeroed, 1)
                sp.wait_ge(mask_stored, settled)
                sp.wait_ge(masked, from_zero((g - 1) * E))
                sp.dma_start(mask_bc[:, u].rearrange("p e t -> p (e t)"),
                             mask_dram[u].rearrange("r q -> (r q)").unsqueeze(0).to_broadcast([P, E * T])
                             ).then_inc(mask_loaded[u], 16)

            def store_out(g, u):
                settled = held(sp, wait_count, g + 1)
                sp.wait_ge(vec_zeroed, 1)
                sp.wait_ge(out_ready, settled)
                sp.dma_start(out_rows[:, bass.ds(g * BG, BG), :],
                             out_sb[:, u].rearrange("p (b k) d -> p b (k d)", k=KT)).then_inc(out_stored[u], 16)

            sp.wait_ge(fw_split, 4)
            spread_mask(0, 0, 0)

            def turn(i, first=False, last=False):
                for u in range(2):
                    g = i * 2 + u
                    if not (first and u == 0):
                        store_out(g - 1, 1 - u)
                    if not (last and u == 1):
                        spread_mask(g + 1, i, 1 - u)

            turn(0, first=True)
            with sp.Fori(1, PAIRS - 1) as i:
                turn(i)
            turn(PAIRS - 1, last=True)
            store_out(G - 1, 1)
            for u in range(2):
                sp.wait_ge(out_stored[u], PAIRS * 16)

        @block.gpsimd
        def _(pool):
            wait_count = ctx.enter_context(pool.register("wait_count"))
            steps = 0

            def const(ins):
                nonlocal steps
                steps += 1
                ins.then_inc(const_ready, 1)

            pool.memset(vec_rows[:], 0.0).then_inc(vec_zeroed, 1)
            const(pool.memset(eye[:], 0.0))
            const(pool.memset(ident[:], 0.0))
            pool.wait_ge(const_ready, steps)
            for k in range(KT):
                const(pool.affine_select(out=eye[:, k, :], in_=eye[:, k, :], compare_op=ALU.not_equal, fill=1.0,
                                         base=k, pattern=[[-1, N]], channel_multiplier=KT))
            const(pool.affine_select(out=ident[:], in_=ident[:], compare_op=ALU.not_equal, fill=1.0,
                                     base=0, pattern=[[-1, P]], channel_multiplier=1))
            const(pool.memset(ones[:], 1.0))
            const(pool.memset(minus_half[:], -0.5))
            for e in range(E):
                const(pool.memset(expert_number[:, :, e], float(e)))
            pool.wait_ge(const_ready, steps)
            const(pool.tensor_copy(ident_bf[:], ident[:]))
            pool.wait_ge(const_ready, steps)
            pool.wait_ge(deg_ready, 1)
            pool.tensor_tensor(dinv[:], deg[:], minus_half[:, 0:KT], ALU.pow).then_inc(dinv_ready, 1)

            def center_tokens(target, g, n, u):
                settled = held(pool, wait_count, n + 1)
                pool.wait_ge(vec_zeroed, 1)
                pool.wait_ge(ln_mv_ready, settled)
                pool.tensor_tensor(target, group_tiles(g), x_mv[:, u, :, 0:1].to_broadcast([P, J, D]),
                                   ALU.subtract).then_inc(ln_centered, 1)
                pool.tensor_scalar(x_var[:, u], x_mv[:, u, :, 1], EPS, None, ALU.add).then_inc(ln_var_step, 1)
                pool.wait_ge(ln_var_step, n + 1)
                pool.tensor_tensor(x_rstd[:, u], x_var[:, u], minus_half[:], ALU.pow).then_inc(ln_rstd_ready, 1)

            def batch_norm_rstd(at, mean_var, count, done):
                pool.wait_ge(bn_mv_ready, done)
                pool.tensor_scalar(bn_var[:, at:at + count], mean_var, EPS, None, ALU.add).then_inc(bn_var_step, 1)
                pool.wait_ge(bn_var_step, done)
                pool.tensor_tensor(bn_rstd[:, at:at + count], bn_var[:, at:at + count], minus_half[:, 0:count],
                                   ALU.pow).then_inc(bn_rstd_ready, 1)

            def center_turn(i):
                for u in range(2):
                    g = i * 2 + u
                    pool.wait_ge(agg_done, from_zero(g - 1))
                    center_tokens(xln[:, u], g, g, u)

            center_turn(0)
            with pool.Fori(1, PAIRS) as i:
                center_turn(i)

            batch_norm_rstd(0, h_mv[:, :, 1], HT, 1)
            pool.wait_ge(fw_loaded, 64)
            for a, b in ((0, W1C), (W1C, W1C + W2C)):
                pool.tensor_copy(fw_hi[:, a:b], fw_raw[:, a:b]).then_inc(fw_split, 1)
            pool.wait_ge(fw_split, 2)
            for a, b in ((0, W1C), (W1C, W1C + W2C)):
                pool.tensor_tensor(fw_lo[:, a:b], fw_raw[:, a:b], fw_hi[:, a:b].bitcast(F32),
                                   ALU.subtract).then_inc(fw_split, 1)
            batch_norm_rstd(HT, y_mv[:, 1:2], 1, 2)

            def norm_x(n, u):
                pool.wait_ge(xt_done, from_zero(n))
                center_tokens(x_norm, n, n + G, u)
                pool.wait_ge(ln_rstd_ready, n + G + 1)
                pool.tensor_tensor(x_norm, x_norm, x_rstd[:, u].unsqueeze(2).to_broadcast([P, J, D]),
                                   ALU.mult).then_inc(x_normed, 1)

            norm_x(0, 0)
            norm_x(1, 1)

            def turn(i, last=False):
                for u in range(2):
                    g = i * 2 + u
                    for e in range(E):
                        if e == 1 and not last:
                            norm_x(g + 2, u)
                        if e >= 1:
                            pool.wait_ge(masked, g * E + e + 1)
                            pool.wait_ge(added, from_zero(g * (E - 1) + e - 1))
                            pool.tensor_tensor(ffn_sum[:, u], ffn_sum[:, u], y_masked[:, e % 2],
                                               ALU.add).then_inc(added, 1)

            turn(0)
            with pool.Fori(1, PAIRS - 1) as i:
                turn(i)
            turn(PAIRS - 1, last=True)

        @block.scalar
        def _(act):
            def evacuate_hidden(g, u):
                act.wait_ge(h1_done, g + 1)
                for k in range(HT):
                    act.activation(group_columns(h1[:, k, :], g), h1_ps[:, u, k, :], ACT.Identity,
                                   bias=column("gb1", k)).then_inc(h1_ready, 1)

            def evacuate_aggregate(g, u):
                act.wait_ge(agg_done, g + 1)
                act.copy(agg_t[:, u], agg_ps[:, u]).then_inc(agg_copied, 1)

            act.wait_ge(weights_turned, 1)
            act.copy(gw_t[:], h1_ps[:, 0, 1, :].rearrange("p (c q) -> p c q", q=P)).then_inc(weights_ready, 1)
            act.wait_ge(weights_turned, 2)
            act.copy(vec[:], h1_ps[:, 0, 0, 0:P]).then_inc(weights_ready, 1)
            act.wait_ge(weights_ready, 2)
            evacuate_aggregate(0, 0)
            evacuate_aggregate(1, 1)
            evacuate_hidden(0, 0)
            with act.Fori(0, PAIRS - 1) as i:
                for u in range(2):
                    evacuate_aggregate(i * 2 + 2 + u, u)
                    evacuate_hidden(i * 2 + 1 + u, 1 - u)
            evacuate_hidden(G - 1, 1)

            act.wait_ge(bn_ready, 1)

            def relu(i):
                for u in range(2):
                    g = i * 2 + u
                    act.wait_ge(y_done, from_zero(g - 1))
                    for k in range(HT):
                        act.activation(h_relu[:, u, k, :], group_columns(h1[:, k, :], g), ACT.Relu,
                                       bias=bn_shift[:, k:k + 1], scale=bn_scale[:, k:k + 1]).then_inc(relu_done, 1)

            relu(0)
            with act.Fori(1, PAIRS) as i:
                relu(i)

            def split_hi_x(n, u):
                act.wait_ge(xt_done, n + 1)
                act.copy(xt_hi[:, u], work_b).then_inc(xt_hi_ready, 1)

            split_hi_x(0, 0)

            def turn(i, last=False):
                for u in range(2):
                    g = i * 2 + u
                    for e in range(E):
                        q = g * E + e
                        r = e % RING
                        for f in range(FT):
                            act.wait_ge(up_done, q * FT + f + 1)
                            if f == 0:
                                act.wait_ge(lo_done, from_zero(q - RING + 1))
                            act.activation(hid[:, r, f, :], hid_ps[:, e % 2, f, :], ACT.Gelu,
                                           bias=column("fb1", e * FT + f)).then_inc(gelu_done, 1)
                        act.wait_ge(gelu_done, (q + 1) * FT)
                        act.wait_ge(down_done, from_zero(q - RING + 1))
                        act.copy(hid_hi[:, r], hid[:, r]).then_inc(hi_done, 1)
                        if e == 1 and not (last and u == 1):
                            split_hi_x(g + 1, 1 - u)

            turn(0)
            with act.Fori(1, PAIRS - 1) as i:
                turn(i)
            turn(PAIRS - 1, last=True)

        @block.vector
        def _(dve):
            wait_count = ctx.enter_context(dve.register("wait_count"))
            dve.wait_ge(const_ready, 5)
            dve.wait_ge(adj_loaded, 16)
            dve.tensor_tensor(adj_sb[:], adj_sb[:], eye[:], ALU.add).then_inc(adj_step, 1)
            dve.wait_ge(adj_step, 1)
            dve.tensor_reduce(row_sum[:], adj_sb[:], AX_X, ALU.add).then_inc(adj_step, 1)
            dve.tensor_tensor(eye_adj[:], adj_sb[:], eye[:], ALU.mult).then_inc(adj_step, 1)
            dve.wait_ge(adj_step, 3)
            dve.tensor_reduce(diag[:], eye_adj[:], AX_X, ALU.add).then_inc(adj_step, 1)
            dve.wait_ge(col_sum_done, 1)
            dve.tensor_tensor(deg[:], work_a[:, 0:KT], row_sum[:], ALU.add).then_inc(adj_step, 1)
            dve.wait_ge(adj_step, 5)
            dve.tensor_tensor(deg[:], deg[:], diag[:], ALU.subtract).then_inc(deg_ready, 1)

            def layer_norm_stats(g, n, u):
                tiles = group_tiles(g)
                for j in range(J):
                    ins = dve.bn_stats(x_stats[:, u, j, :], tiles[:, j, :])
                ins.then_inc(ln_stats_step, 1)
                settled = held(dve, wait_count, n + 1)
                dve.wait_ge(vec_zeroed, 1)
                dve.wait_ge(ln_stats_step, settled)
                for j in range(J):
                    ins = dve.bn_aggr(x_mv[:, u, j, :], x_stats[:, u, j, :])
                ins.then_inc(ln_mv_ready, 1)

            def hidden_stats(g):
                settled = held(dve, wait_count, g * HT + HT)
                dve.wait_ge(vec_zeroed, 1)
                dve.wait_ge(h1_ready, settled)
                for k in range(HT):
                    ins = dve.bn_stats(h_stats[:, k, bass.ds(g, 1), :].rearrange("p a s -> p (a s)"),
                                       group_columns(h1[:, k, :], g))
                ins.then_inc(h1_counted, 1)

            dve.wait_ge(dinv_ready, 1)
            for k in range(KT):
                dve.tensor_scalar(adj_sb[:, k, :], adj_sb[:, k, :], dinv[:, k:k + 1], None,
                                  ALU.mult).then_inc(adj_scaled, 1)
            dve.wait_ge(x_loaded, 2)
            layer_norm_stats(0, 0, 0)
            layer_norm_stats(1, 1, 1)
            dve.wait_ge(adj_turned, 1)
            for k in range(KT):
                dve.tensor_scalar(a_t[:, k, :], work_b[:, k * N:(k + 1) * N], dinv[:, k:k + 1], None,
                                  ALU.mult).then_inc(a_t_ready, 1)

            def gnn_turn(i, first=False, last=False):
                for u in range(2):
                    g = i * 2 + u
                    dve.wait_ge(ln_rstd_ready, g + 1)
                    dve.tensor_tensor(xln[:, u], xln[:, u], x_rstd[:, u].unsqueeze(2).to_broadcast([P, J, D]),
                                      ALU.mult).then_inc(xln_ready, 1)
                    if not last:
                        settled = held(dve, wait_count, g + 3)
                        dve.wait_ge(vec_zeroed, 1)
                        dve.wait_ge(x_loaded, settled)
                        layer_norm_stats(g + 2, g + 2, u)
                    if not first:
                        hidden_stats(g - 2)

            gnn_turn(0, first=True)
            with dve.Fori(1, PAIRS - 1) as i:
                gnn_turn(i)
            gnn_turn(PAIRS - 1, last=True)
            hidden_stats(G - 2)
            hidden_stats(G - 1)

            def batch_norm(at, count, mean, gamma, beta, done):
                dve.wait_ge(bn_rstd_ready, done)
                c = slice(at, at + count)
                dve.tensor_tensor(bn_scale[:, c], bn_rstd[:, c], gamma, ALU.mult).then_inc(bn_step, 1)
                dve.wait_ge(bn_step, from_zero(2 * done - 1))
                dve.tensor_tensor(bn_mean_scaled[:, c], mean, bn_scale[:, c], ALU.mult).then_inc(bn_step, 1)
                dve.wait_ge(bn_step, 2 * done)
                dve.tensor_tensor(bn_shift[:, c], beta, bn_mean_scaled[:, c], ALU.subtract).then_inc(bn_ready, 1)

            dve.wait_ge(h1_counted, G)
            for k in range(HT):
                ins = dve.bn_aggr(h_mv[:, k, :], h_stats[:, k].rearrange("p g s -> p (g s)"))
            ins.then_inc(bn_mv_ready, 1)
            batch_norm(0, HT, h_mv[:, :, 0], vec[:, names["gg1"]:names["gg1"] + HT],
                       vec[:, names["gbe1"]:names["gbe1"] + HT], 1)
            dve.wait_ge(fw_loaded, 64)
            dve.tensor_copy(wg_parts[:, 0, :], wg_raw[:]).then_inc(wg_split, 1)
            dve.wait_ge(wg_split, 1)
            dve.tensor_tensor(wg_parts[:, 1, :], wg_raw[:], wg_parts[:, 0, :].bitcast(F32),
                              ALU.subtract).then_inc(wg_split, 1)

            with dve.Fori(0, PAIRS) as i:
                for u in range(2):
                    g = i * 2 + u
                    dve.wait_ge(y_done, g + 1)
                    dve.tensor_scalar(group_columns(y, g), y_ps[:, u], column("gb2"), None,
                                      ALU.add).then_inc(y_ready, 1)
                    settled = held(dve, wait_count, g + 1)
                    dve.wait_ge(vec_zeroed, 1)
                    dve.wait_ge(y_ready, settled)
                    dve.bn_stats(y_stats[:, bass.ds(g, 1), :].rearrange("p a s -> p (a s)"),
                                 group_columns(y, g)).then_inc(y_counted, 1)
            dve.wait_ge(y_counted, G)
            dve.bn_aggr(y_mv[:], y_stats[:].rearrange("p g s -> p (g s)")).then_inc(bn_mv_ready, 1)
            batch_norm(HT, 1, y_mv[:, 0:1], column("gg2"), column("gbe2"), 2)
            dve.wait_ge(bn_ready, 2)

            def norm_y(n):
                dve.wait_ge(y_turned, from_zero(n))
                dve.tensor_scalar(y_norm, group_columns(y, n), bn_scale[:, HT:HT + 1], bn_shift[:, HT:HT + 1],
                                  ALU.mult, ALU.add).then_inc(y_normed, 1)

            def add_residual(n):
                dve.wait_ge(y_turned, n + 1)
                tiles = group_tiles(n)
                dve.tensor_tensor(tiles, work_a.rearrange("p (j d) -> p j d", j=J), tiles, ALU.add).then_inc(x2_ready, 1)

            def second_norm_stats(n, u):
                settled = held(dve, wait_count, n + 1)
                dve.wait_ge(vec_zeroed, 1)
                dve.wait_ge(x2_ready, settled)
                layer_norm_stats(n, n + G, u)

            def split_lo_x(n, u):
                dve.wait_ge(xt_hi_ready, n + 1)
                dve.tensor_tensor(xt_lo[:, u], work_b, xt_hi[:, u].bitcast(F32), ALU.subtract).then_inc(xt_lo_ready, 1)

            def pick_experts(n):
                dve.wait_ge(gate_done, n + 1)
                scores = work_a[:, 0:J * 2 * E].rearrange("p (j h e) -> p j h e", j=J, h=2)
                bias = bg_sb[:].unsqueeze(1).to_broadcast([P, J, E])
                dve.tensor_tensor(gate[:], scores[:, :, 0, :], bias, ALU.add).then_inc(gate_step, 1)
                dve.wait_ge(gate_step, n * PICK_STEPS + 1)
                dve.tensor_tensor(gate[:], scores[:, :, 1, :], gate[:], ALU.add).then_inc(gate_step, 1)
                settled = held(dve, wait_count, n * PICK_STEPS + 2)
                dve.wait_ge(vec_zeroed, 1)
                dve.wait_ge(gate_step, settled)
                for j in range(J):
                    ins = dve.max(gate_max[:, j, :], gate[:, j, :])
                ins.then_inc(gate_step, 1)
                settled = held(dve, wait_count, n * PICK_STEPS + 3)
                dve.wait_ge(vec_zeroed, 1)
                dve.wait_ge(gate_step, settled)
                for j in range(J):
                    ins = dve.max_index(gate_idx[:, j, :], gate_max[:, j, :], gate[:, j, :])
                ins.then_inc(gate_step, 1)
                dve.wait_ge(gate_step, n * PICK_STEPS + 4)
                for k in range(2):
                    ins = dve.tensor_tensor(picked[:, k], expert_number[:],
                                            gate_idx[:, :, k:k + 1].to_broadcast([P, J, E]), ALU.is_equal)
                ins.then_inc(gate_step, 1)
                dve.wait_ge(gate_step, n * PICK_STEPS + 5)
                dve.wait_ge(mask_turned, from_zero(n))
                dve.tensor_tensor(mask[:].rearrange("p e j -> p j e"), picked[:, 0], picked[:, 1],
                                  ALU.add).then_inc(mask_ready, 1)

            def copy_mask(n):
                dve.wait_ge(mask_turned, n + 1)
                dve.wait_ge(mask_stored, from_zero(n * 16))
                dve.tensor_copy(mask_t[:], work_b[0:E * J, 0:P]).then_inc(mask_t_ready, 1)

            def mask_expert(g, e, i, u):
                q = g * E + e
                dve.wait_ge(down_done, q + 1)
                if e == 0:
                    dve.wait_ge(mask_loaded[u], i * 16 + 16)
                    dve.wait_ge(sum_turned, from_zero(g - 1))
                    target = ffn_sum[:, u]
                else:
                    dve.wait_ge(added, from_zero(g * (E - 1) + (e - 2 if e > 2 else 0)))
                    target = y_masked[:, e % 2]
                dve.scalar_tensor_tensor(out=target, in0=ffn_ps[:, e % 2], scalar=column("fb2", e),
                                         in1=mask_bc[:, u, e, :], op0=ALU.add, op1=ALU.mult).then_inc(masked, 1)

            def split_lo_hidden(g, e):
                q = g * E + e
                dve.wait_ge(hi_done, q + 1)
                dve.wait_ge(down_done, from_zero(q - RING + 1))
                r = e % RING
                dve.tensor_tensor(hid_lo[:, r], hid[:, r], hid_hi[:, r].bitcast(F32),
                                  ALU.subtract).then_inc(lo_done, 1)

            def finish(o, i, u):
                dve.wait_ge(sum_turned, o + 1)
                dve.wait_ge(out_stored[u], from_zero(i * 16))
                dve.tensor_tensor(out_sb[:, u], work_b.rearrange("p (j d) -> p j d", j=J), group_tiles(o),
                                  ALU.add).then_inc(out_ready, 1)

            norm_y(0)
            norm_y(1)
            add_residual(0)
            second_norm_stats(0, 0)
            add_residual(1)
            second_norm_stats(1, 1)
            split_lo_x(0, 0)

            def turn(i, first=False, last=False):
                for u in range(2):
                    g = i * 2 + u
                    start = first and u == 0
                    prepare = not (last and u == 1)
                    for e in range(E):
                        if e >= LAG:
                            mask_expert(g, e - LAG, i, u)
                        elif not start:
                            mask_expert(g - 1, E - LAG + e, i if u else i - 1, 1 - u)
                        if e == 0 and not last:
                            norm_y(g + 2)
                        if e == 2 and not last:
                            add_residual(g + 2)
                        if e == 3 and not last:
                            second_norm_stats(g + 2, u)
                        if e == 4 and prepare:
                            pick_experts(g + 1)
                        if e == 5 and not start:
                            finish(g - 1, i if u else i - 1, 1 - u)
                        if e == 7 and prepare:
                            copy_mask(g + 1)
                        split_lo_hidden(g, e)
                        if e == 0 and start:
                            pick_experts(0)
                        if e == 1 and start:
                            copy_mask(0)
                        if e == 1 and prepare:
                            split_lo_x(g + 1, 1 - u)

            turn(0, first=True)
            with dve.Fori(1, PAIRS - 1) as i:
                turn(i)
            turn(PAIRS - 1, last=True)
            for e in range(E - LAG, E):
                mask_expert(G - 1, e, PAIRS - 1, 1)
            finish(G - 1, PAIRS - 1, 1)

        @block.tensor
        def _(pe):
            def turn_tiles(target, source, count):
                for j in range(count):
                    ins = pe.transpose(target[:, j * P:(j + 1) * P], source(j), ident[:])
                return ins

            pe.wait_ge(const_ready, 16)
            pe.wait_ge(adj_step, 1)
            for k in range(KT):
                for l in range(KT):
                    ins = pe.matmul(work_a[:, k:k + 1], adj_sb[:, l, k::KT], ones[:, 0:1],
                                    start=(l == 0), stop=(l == KT - 1))
            ins.then_inc(col_sum_done, 1)
            pe.wait_ge(adj_scaled, KT)
            ins = turn_tiles(work_b, lambda c: adj_sb[:, c % KT, (c // KT)::KT], KT * KT)
            ins.then_inc(adj_turned, 1)
            pe.wait_ge(gw_loaded, 32)
            ins = turn_tiles(h1_ps[:, 0, 1, :],
                             lambda c: gw1_raw[:, c, :] if c < HT else gw2_raw[:, (c - HT) * P:(c - HT + 1) * P], 2 * HT)
            ins.then_inc(weights_turned, 1)
            pe.wait_ge(vec_loaded, 8 * 16)
            pe.transpose(h1_ps[:, 0, 0, 0:P], vec_rows[:], ident[:]).then_inc(weights_turned, 1)
            pe.wait_ge(a_t_ready, KT)
            pe.wait_ge(weights_ready, 2)

            def aggregate(g, u):
                pe.wait_ge(xln_ready, g + 1)
                pe.wait_ge(agg_copied, from_zero(g - 1))
                for b in range(BG):
                    for k in range(KT):
                        ins = pe.matmul(agg_ps[:, u, b * N:(b + 1) * N], xln[:, u, b * KT + k, :], a_t[:, k, :],
                                        start=(k == 0), stop=(k == KT - 1))
                ins.then_inc(agg_done, 1)

            def hidden(g, u):
                pe.wait_ge(agg_copied, g + 1)
                pe.wait_ge(h1_ready, from_zero((g - 1) * HT))
                for k in range(HT):
                    ins = pe.matmul(h1_ps[:, u, k, :], gw_t[:, k, :], agg_t[:, u], start=True, stop=True)
                ins.then_inc(h1_done, 1)

            aggregate(0, 0)
            aggregate(1, 1)
            hidden(0, 0)
            aggregate(2, 0)
            hidden(1, 1)
            with pe.Fori(1, PAIRS - 1) as i:
                for u in range(2):
                    aggregate(i * 2 + 1 + u, 1 - u)
                    hidden(i * 2 + u, u)
            aggregate(G - 1, 1)
            hidden(G - 2, 0)
            hidden(G - 1, 1)

            def second_layer(i):
                for u in range(2):
                    g = i * 2 + u
                    pe.wait_ge(relu_done, g * HT + HT)
                    pe.wait_ge(y_ready, from_zero(g - 1))
                    for k in range(HT):
                        ins = pe.matmul(y_ps[:, u], gw_t[:, HT + k, :], h_relu[:, u, k, :],
                                        start=(k == 0), stop=(k == HT - 1))
                    ins.then_inc(y_done, 1)

            second_layer(0)
            with pe.Fori(1, PAIRS) as i:
                second_layer(i)

            def turn_y(n):
                pe.wait_ge(y_normed, n + 1)
                if isinstance(n, int) and n < 2:
                    pe.wait_ge(x2_ready, n)
                else:
                    pe.wait_ge(gate_step, (n - 2) * PICK_STEPS + 2)
                turn_tiles(work_a, lambda j: y_norm[:, j * P:(j + 1) * P], J).then_inc(y_turned, 1)

            def turn_x(n):
                pe.wait_ge(x_normed, n + 1)
                pe.wait_ge(mask_t_ready, from_zero(n))
                turn_tiles(work_b, lambda j: x_norm[:, j, :], J).then_inc(xt_done, 1)

            def gate_scores(n, u):
                pe.wait_ge(xt_lo_ready, n + 1)
                pe.wait_ge(x2_ready, min(n + 2, G) if isinstance(n, int) else n + 2)
                parts = wg_parts[:].rearrange("p h e -> p (h e)")
                for j in range(J):
                    c = slice(j * P, (j + 1) * P)
                    o = work_a[:, j * 2 * E:(j + 1) * 2 * E]
                    pe.matmul(o, xt_hi[:, u, c], parts, start=True, stop=False)
                    ins = pe.matmul(o, xt_lo[:, u, c], parts, start=False, stop=True)
                ins.then_inc(gate_done, 1)

            def turn_mask(n):
                pe.wait_ge(mask_ready, n + 1)
                pe.wait_ge(out_ready, from_zero(n - 1))
                pe.matmul(work_b[0:E * J, 0:P], mask[:].rearrange("p e j -> p (e j)"), ident_bf[:],
                          start=True, stop=True).then_inc(mask_turned, 1)

            def turn_sum(o, u):
                pe.wait_ge(added, (o + 1) * (E - 1))
                if isinstance(o, int) and o == G - 1:
                    pe.wait_ge(out_ready, G - 1)
                elif isinstance(o, int) and o == G - 2:
                    pe.wait_ge(mask_t_ready, G)
                else:
                    pe.wait_ge(xt_lo_ready, o + 3)
                turn_tiles(work_b, lambda j: ffn_sum[:, u, j * P:(j + 1) * P], J).then_inc(sum_turned, 1)

            def up(g, e, u):
                q = g * E + e
                if e == 0:
                    pe.wait_ge(xt_lo_ready, g + 1)
                pe.wait_ge(gelu_done, from_zero((q - 1) * FT))
                for f in range(FT):
                    o = hid_ps[:, e % 2, f, :]
                    pe.matmul(o, w1(fw_hi, e, f), xt_hi[:, u], start=True, stop=False)
                    pe.matmul(o, w1(fw_hi, e, f), xt_lo[:, u], start=False, stop=False)
                    pe.matmul(o, w1(fw_lo, e, f), xt_hi[:, u], start=False, stop=True).then_inc(up_done, 1)

            def down(g, e):
                q = g * E + e
                pe.wait_ge(lo_done, q + 1)
                pe.wait_ge(masked, from_zero(q - 1))
                o = ffn_ps[:, e % 2]
                for f in range(FT):
                    pe.matmul(o, w2(fw_hi, e, f), hid_hi[:, e % RING, f, :], start=(f == 0), stop=False)
                    pe.matmul(o, w2(fw_hi, e, f), hid_lo[:, e % RING, f, :], start=False, stop=False)
                    ins = pe.matmul(o, w2(fw_lo, e, f), hid_hi[:, e % RING, f, :], start=False, stop=(f == FT - 1))
                ins.then_inc(down_done, 1)

            turn_y(0)
            turn_y(1)
            turn_x(0)
            pe.wait_ge(wg_split, 2)
            pe.wait_ge(fw_split, 4)

            def turn(i, first=False, last=False):
                for u in range(2):
                    g = i * 2 + u
                    start = first and u == 0
                    prepare = not (last and u == 1)
                    for e in range(E):
                        up(g, e, u)
                        if e == 0 and start:
                            gate_scores(0, 0)
                        if e == 1 and start:
                            turn_mask(0)
                        if e == 1 and prepare:
                            turn_x(g + 1)
                        if e == 2 and not last:
                            turn_y(g + 2)
                        if e == 4 and prepare:
                            gate_scores(g + 1, 1 - u)
                        if e == 5 and not start:
                            turn_sum(g - 1, 1 - u)
                        if e == 7 and prepare:
                            turn_mask(g + 1)
                        if e >= LAG:
                            down(g, e - LAG)
                        elif not start:
                            down(g - 1, E - LAG + e)

            turn(0, first=True)
            with pe.Fori(1, PAIRS - 1) as i:
                turn(i)
            turn(PAIRS - 1, last=True)
            for e in range(E - LAG, E):
                down(G - 1, e)
            turn_sum(G - 1, 1)


_INS = ["x", "adj", "L0_gnn_W1", "L0_gnn_b1", "L0_gnn_g1", "L0_gnn_be1", "L0_gnn_W2", "L0_gnn_b2", "L0_gnn_g2",
        "L0_gnn_be2", "L0_ffn_Wg", "L0_ffn_bg", "L0_ffn_W1", "L0_ffn_b1", "L0_ffn_W2", "L0_ffn_b2"]


def kernel(**inputs):
    import numpy as _np
    import concourse.bacc as _bacc
    from concourse import mybir as _mybir
    from concourse.bass_utils import run_bass_kernel_spmd as _run

    nc = _bacc.Bacc("TRN2", target_bir_lowering=False, num_devices=1)
    arrays, args = {}, []
    for name in _INS:
        a = _np.ascontiguousarray(inputs[name])
        arrays[f"in_{name}_dram"] = a
        args.append(nc.dram_tensor(f"in_{name}_dram", a.shape, _mybir.dt.from_np(a.dtype), kind="ExternalInput").ap())
    shape = inputs["x"].shape
    out = nc.dram_tensor("out_0_dram", shape, _mybir.dt.float32, kind="ExternalOutput").ap()
    gnn_moe_program(nc, *args, out)
    r = _run(nc, [arrays], core_ids=[0])
    return r.results[0]["out_0_dram"]
```

```python
from contextlib import ExitStack

import concourse.bass as bass
from concourse import mybir

F32 = mybir.dt.float32
F32R = mybir.dt.float32r
BF16 = mybir.dt.bfloat16
U32 = mybir.dt.uint32
ALU = mybir.AluOpType
ACT = mybir.ActivationFunctionType
AX_X = mybir.AxisListType.X

P = 128
EPS = 1e-5


def from_zero(value):
    return max(value, 0) if isinstance(value, int) else value


def held(engine, register, value):
    if isinstance(value, int):
        return value
    engine.reg_mov(register, value)
    return register


def gnn_moe_program(nc, x, adj, gw1, gb1, gg1, gbe1, gw2, gb2, gg2, gbe2, wg, bg, fw1, fb1, fw2, fb2, out):
    B, N, D = x.shape
    H = gw1.shape[0]
    E, _, FH = fw1.shape
    KT = N // P
    HT = H // P
    FT = FH // P
    BG = 2
    G = B // BG
    T = BG * N
    J = T // P
    PAIRS = G // 2
    LOADS = 8
    LAG = 3
    AHEAD = 6
    RING = 4
    PICK_STEPS = 5
    assert D == P and KT == 2 and HT == 2 and FT == 2 and T == 512 and G % LOADS == 0

    x_rows = x.rearrange("b (p k) d -> p b (k d)", k=KT)
    out_rows = out.rearrange("b (p k) d -> p b (k d)", k=KT)

    with ExitStack() as ctx:
        def sb(name, shape, dt):
            return ctx.enter_context(nc.sbuf_tensor(name, shape, dt))

        def sem(name):
            return ctx.enter_context(nc.semaphore(name))

        x_sb = sb("x_sb", [P, G * J, D], F32)
        h1 = sb("h1", [P, HT, G * T], F32)
        y = h1[:, 0, :]
        spare = h1[:, 1, :]
        ident = sb("ident", [P, P], F32)
        ident_bf = sb("ident_bf", [P, P], BF16)
        ones = sb("ones", [P, 2], F32)
        minus_half = sb("minus_half", [P, 2 * J], F32)
        expert_number = sb("expert_number", [P, J, E], F32)

        adj_sb = sb("adj_sb", [P, KT, N], F32)
        eye = sb("eye", [P, KT, N], F32)
        eye_bf = eye[:].rearrange("p k m -> p (k m)").bitcast(BF16)[:, 0:T]
        eye_adj = h1[:, 1, 0:KT * N].rearrange("p (k m) -> p k m", k=KT)
        gw1_raw = h1[:, 1, T:T + HT * D].rearrange("p (k d) -> p k d", k=HT)
        gw2_raw = h1[:, 1, 2 * T:2 * T + H]
        a_t = sb("a_t", [P, KT, N], F32)
        row_sum = sb("row_sum", [P, KT], F32)
        diag = sb("diag", [P, KT], F32)
        deg = sb("deg", [P, KT], F32)
        dinv = sb("dinv", [P, KT], F32)

        NV = 3 * HT + 3 + E * FT + E
        vec_rows = sb("vec_rows", [P, P], F32)
        vec = sb("vec", [P, P], F32)
        names, at = {}, 0
        for name, rows in (("gb1", HT), ("gg1", HT), ("gbe1", HT), ("gb2", 1), ("gg2", 1), ("gbe2", 1),
                            ("fb1", E * FT), ("fb2", E)):
            names[name] = at
            at += rows
        assert at == NV

        def column(name, k=0):
            return vec[:, names[name] + k:names[name] + k + 1]

        gw1_hi = sb("gw1_hi", [P, HT, P], F32R)
        gw1_lo = sb("gw1_lo", [P, HT, P], F32R)
        gw2_t = sb("gw2_t", [P, HT, P], F32)
        bg_sb = sb("bg_sb", [P, E], F32)
        wg_raw = sb("wg_raw", [P, E], F32)
        wg_parts = sb("wg_parts", [P, 2, E], F32R)

        W1C = E * FH
        W2C = E * FT * D
        fw_raw = sb("fw_raw", [P, W1C + W2C], F32)
        fw_hi = sb("fw_hi", [P, W1C + W2C], F32R)
        fw_lo = sb("fw_lo", [P, W1C + W2C], F32R)
        mask_bc = fw_raw[:].bitcast(BF16)[:, 0:2 * E * T].rearrange("p (u e t) -> p u e t", u=2, e=E)

        def w1(part, e, f):
            return part[:, e * FH + f * P:e * FH + (f + 1) * P]

        def w2(part, e, f):
            at = W1C + (e * FT + f) * D
            return part[:, at:at + D]

        phase_buf = sb("phase_buf", [P, 4 * T], F32)
        xln = phase_buf[:, 0:2 * T].rearrange("p (u j d) -> p u j d", u=2, j=J)
        h_relu = phase_buf[:, :].rearrange("p (u k t) -> p u k t", u=2, k=HT)
        x_stats = sb("x_stats", [P, 2, J, 6], F32)
        x_mv = sb("x_mv", [P, 2, J, 2], F32)
        zero_eps = sb("zero_eps", [P, J, 2], F32)
        gnn_mv = sb("gnn_mv", [P, G, J, 2], F32)
        x_var = sb("x_var", [P, 2, J], F32)
        x_rstd = sb("x_rstd", [P, 2, J], F32)
        start_rstd = sb("start_rstd", [P, 2, J], F32)
        h_stats = sb("h_stats", [P, HT, G, 6], F32)
        h_mv = sb("h_mv", [P, HT, 2], F32)
        y_stats = sb("y_stats", [P, G, 6], F32)
        y_mv = sb("y_mv", [P, 2], F32)
        bn_var = sb("bn_var", [P, HT + 1], F32)
        bn_rstd = sb("bn_rstd", [P, HT + 1], F32)
        bn_scale = sb("bn_scale", [P, HT + 1], F32)
        bn_shift = sb("bn_shift", [P, HT + 1], F32)
        bn_mean_scaled = sb("bn_mean_scaled", [P, HT + 1], F32)

        at = 0

        def carve(count):
            nonlocal at
            at += count
            assert at <= G * T
            return spare[:, at - count:at]

        y_norm = carve(T)
        x_norm = carve(T).rearrange("p (j d) -> p j d", j=J)
        hid = carve(RING * FT * T).rearrange("p (r f t) -> p r f t", r=RING, f=FT)
        y_masked = carve(2 * T).rearrange("p (r t) -> p r t", r=2)
        ffn_sum = carve(2 * T).rearrange("p (u t) -> p u t", u=2)
        out_sb = carve(2 * T).rearrange("p (u j d) -> p u j d", u=2, j=J)
        xt_hi = sb("xt_hi", [P, 2, T], F32R)
        xt_lo = sb("xt_lo", [P, 2, T], F32R)
        agg_hi, agg_lo = xt_hi, xt_lo
        hid_hi = sb("hid_hi", [P, RING, FT, T], F32R)
        hid_lo = sb("hid_lo", [P, RING, FT, T], F32R)
        gate = sb("gate", [P, J, E], F32)
        gate_max = sb("gate_max", [P, J, 8], F32)
        gate_idx = sb("gate_idx", [P, J, 8], U32)
        picked = sb("picked", [P, 2, J, E], F32)
        mask = sb("mask", [P, E, J], BF16)
        mask_t = sb("mask_t", [E * J, P], BF16)
        mask_dram = nc.dram_tensor("mask_dram", (2, E * J, P), BF16).ap()

        psum = ctx.enter_context(nc.psum_tensor("psum", [P, 8, T], F32))
        agg_ps = psum[:, 0:2, :]
        h1_ps = psum[:, 2:6, :].rearrange("p (u k) t -> p u k t", u=2)
        weights_ps = h1_ps[:, 0, 1, :].rearrange("p (c q) -> p c q", q=P)
        y_ps = psum[:, 6:8, :]
        hid_ps = psum[:, 0:4, :].rearrange("p (r f) t -> p r f t", r=2)
        ffn_ps = psum[:, 4:6, :]
        last_out_ps = psum[:, 0:J, 0:D]
        work_a = psum[:, 6, :]
        work_b = psum[:, 7, :]

        const_ready = sem("const_ready")
        adj_loaded = sem("adj_loaded")
        vec_zeroed = sem("vec_zeroed")
        vec_loaded = sem("vec_loaded")
        gw_loaded = sem("gw_loaded")
        fw_loaded = sem("fw_loaded")
        x_load = [sem(f"x_load{i}") for i in range(LOADS)]
        x_loaded = sem("x_loaded")
        adj_step = sem("adj_step")
        deg_ready = sem("deg_ready")
        dinv_ready = sem("dinv_ready")
        col_sum_done = sem("col_sum_done")
        adj_scaled = sem("adj_scaled")
        adj_turned = sem("adj_turned")
        gw1_lo_ready = sem("gw1_lo_ready")
        a_t_ready = sem("a_t_ready")
        weights_turned = sem("weights_turned")
        weights_ready = sem("weights_ready")
        wg_split = sem("wg_split")
        fw_split = sem("fw_split")
        ln_stats_step = sem("ln_stats_step")
        ln_mv_step = sem("ln_mv_step")
        gnn_mv_ready = sem("gnn_mv_ready")
        ln_centered = sem("ln_centered")
        ln_var_step = sem("ln_var_step")
        ln_rstd_ready = sem("ln_rstd_ready")
        xln_ready = sem("xln_ready")
        act_scaled = sem("act_scaled")
        agg_done = sem("agg_done")
        agg_hi_ready = sem("agg_hi_ready")
        agg_lo_ready = sem("agg_lo_ready")
        h1_done = sem("h1_done")
        h1_ready = sem("h1_ready")
        h1_counted = sem("h1_counted")
        bn_mv_ready = sem("bn_mv_ready")
        bn_var_step = sem("bn_var_step")
        bn_rstd_ready = sem("bn_rstd_ready")
        bn_step = sem("bn_step")
        bn_ready = sem("bn_ready")
        relu_done = sem("relu_done")
        y_done = sem("y_done")
        y_ready = sem("y_ready")
        y_counted = sem("y_counted")
        y_normed = sem("y_normed")
        y_turned = sem("y_turned")
        x2_ready = sem("x2_ready")
        first_x_normed = sem("first_x_normed")
        x_normed = sem("x_normed")
        xt_done = sem("xt_done")
        xt_hi_ready = sem("xt_hi_ready")
        xt_lo_ready = sem("xt_lo_ready")
        gate_done = sem("gate_done")
        gate_step = sem("gate_step")
        mask_ready = sem("mask_ready")
        mask_turned = sem("mask_turned")
        mask_t_ready = sem("mask_t_ready")
        mask_stored = sem("mask_stored")
        mask_loaded = [sem(f"mask_loaded{u}") for u in range(2)]
        up_done = sem("up_done")
        gelu_done = sem("gelu_done")
        hi_done = sem("hi_done")
        lo_done = sem("lo_done")
        down_done = sem("down_done")
        masked = sem("masked")
        added = sem("added")
        sum_turned = sem("sum_turned")
        out_ready = sem("out_ready")
        out_stored = [sem(f"out_stored{u}") for u in range(2)]

        block = ctx.enter_context(nc.Block())

        def group_tiles(g):
            return x_sb[:, bass.ds(g * J, J), :]

        def group_columns(buf, g):
            return buf[:, bass.ds(g * T, T)]

        @block.sync
        def _(sp):
            wait_count = ctx.enter_context(sp.register("wait_count"))
            per = B // LOADS

            def load_x(i):
                sp.dma_start(x_sb[:, i * per * KT:(i + 1) * per * KT, :].rearrange("p (b k) d -> p b (k d)", k=KT),
                             x_rows[:, i * per:(i + 1) * per, :]).then_inc(x_load[i], 16)

            sp.dma_start(adj_sb[:], adj.rearrange("(p k) m -> p k m", k=KT)).then_inc(adj_loaded, 16)
            load_x(0)
            load_x(1)
            sp.wait_ge(vec_zeroed, 1)
            for name, source in (("gb1", gb1), ("gg1", gg1), ("gbe1", gbe1), ("gb2", gb2), ("gg2", gg2), ("gbe2", gbe2)):
                rows = source.shape[0] // P
                sp.dma_start(vec_rows[names[name]:names[name] + rows, :],
                              source.rearrange("(k p) -> k p", p=P)).then_inc(vec_loaded, 16)
            sp.dma_start(vec_rows[names["fb1"]:names["fb1"] + E * FT, :],
                          fb1.rearrange("e (f p) -> (e f) p", p=P)).then_inc(vec_loaded, 16)
            sp.dma_start(vec_rows[names["fb2"]:names["fb2"] + E, :], fb2).then_inc(vec_loaded, 16)
            for i in range(2, LOADS):
                load_x(i)
            sp.dma_start(wg_raw[:], wg).then_inc(fw_loaded, 16)
            sp.dma_start(bg_sb[:], bg.unsqueeze(0).to_broadcast([P, E])).then_inc(fw_loaded, 16)
            sp.dma_start(fw_raw[:, 0:W1C].rearrange("p (e h) -> p e h", e=E),
                         fw1.rearrange("e d h -> d e h")).then_inc(fw_loaded, 16)
            sp.dma_start(fw_raw[:, W1C:W1C + W2C].rearrange("p (e f d) -> p e f d", e=E, f=FT),
                         fw2.rearrange("e (f p) d -> p e f d", p=P)).then_inc(fw_loaded, 16)
            for i in range(LOADS):
                sp.wait_ge(x_load[i], 16)
                sp.sem_inc(x_loaded, G // LOADS)

            def spread_mask(g, i, u):
                sp.wait_ge(mask_t_ready, g + 1)
                sp.dma_start(mask_dram[u], mask_t[:]).then_inc(mask_stored, 16)
                settled = held(sp, wait_count, g * 16 + 16)
                sp.wait_ge(vec_zeroed, 1)
                sp.wait_ge(mask_stored, settled)
                sp.wait_ge(masked, from_zero((g - 1) * E))
                sp.dma_start(mask_bc[:, u].rearrange("p e t -> p (e t)"),
                             mask_dram[u].rearrange("r q -> (r q)").unsqueeze(0).to_broadcast([P, E * T])
                             ).then_inc(mask_loaded[u], 16)

            def store_out(g, u):
                settled = held(sp, wait_count, g + 1)
                sp.wait_ge(vec_zeroed, 1)
                sp.wait_ge(out_ready, settled)
                sp.dma_start(out_rows[:, bass.ds(g * BG, BG), :],
                             out_sb[:, u].rearrange("p (b k) d -> p b (k d)", k=KT)).then_inc(out_stored[u], 16)

            sp.wait_ge(fw_split, 4)
            spread_mask(0, 0, 0)

            def turn(i, first=False, last=False):
                for u in range(2):
                    g = i * 2 + u
                    if not (first and u == 0):
                        store_out(g - 1, 1 - u)
                    if not (last and u == 1):
                        spread_mask(g + 1, i, 1 - u)

            turn(0, first=True)
            with sp.Fori(1, PAIRS - 1) as i:
                turn(i)
            turn(PAIRS - 1, last=True)
            store_out(G - 1, 1)
            for u in range(2):
                sp.wait_ge(out_stored[u], PAIRS * 16)

        @block.gpsimd
        def _(pool):
            wait_count = ctx.enter_context(pool.register("wait_count"))
            steps = 0

            def const(ins):
                nonlocal steps
                steps += 1
                ins.then_inc(const_ready, 1)

            pool.memset(vec_rows[:], 0.0).then_inc(vec_zeroed, 1)
            const(pool.memset(eye[:], 0.0))
            const(pool.memset(ident[:], 0.0))
            pool.wait_ge(const_ready, steps)
            for k in range(KT):
                const(pool.affine_select(out=eye[:, k, :], in_=eye[:, k, :], compare_op=ALU.not_equal, fill=1.0,
                                         base=k, pattern=[[-1, N]], channel_multiplier=KT))
            const(pool.affine_select(out=ident[:], in_=ident[:], compare_op=ALU.not_equal, fill=1.0,
                                     base=0, pattern=[[-1, P]], channel_multiplier=1))
            const(pool.memset(ones[:], 1.0))
            const(pool.memset(minus_half[:], -0.5))
            const(pool.memset(zero_eps[:, :, 0], 0.0))
            const(pool.memset(zero_eps[:, :, 1], EPS))
            for e in range(E):
                const(pool.memset(expert_number[:, :, e], float(e)))
            pool.wait_ge(const_ready, steps)
            const(pool.tensor_copy(ident_bf[:], ident[:]))
            pool.wait_ge(const_ready, steps)
            pool.wait_ge(deg_ready, 1)
            pool.tensor_tensor(dinv[:], deg[:], minus_half[:, 0:KT], ALU.pow).then_inc(dinv_ready, 1)

            def first_rstd(i):
                settled = held(pool, wait_count, i * 2 + 2)
                pool.wait_ge(vec_zeroed, 1)
                pool.wait_ge(gnn_mv_ready, settled)
                if not (isinstance(i, int) and i < 2):
                    pool.wait_ge(xln_ready, i * 2 - 2)
                    pool.wait_ge(act_scaled, i * 2)
                pool.tensor_tensor(x_rstd[:], gnn_mv[:, bass.ds(i * 2, 2), :, 1],
                                   minus_half[:].rearrange("p (u j) -> p u j", u=2),
                                   ALU.pow).then_inc(ln_rstd_ready, 1)

            def center_tokens(g, u):
                settled = held(pool, wait_count, from_zero(g - 1))
                pool.wait_ge(vec_zeroed, 1)
                pool.wait_ge(agg_done, settled)
                mean = gnn_mv[:, bass.ds(g, 1), :, 0:1].rearrange("p a j m -> p (a j) m")
                pool.tensor_tensor(xln[:, u], group_tiles(g), mean.to_broadcast([P, J, D]),
                                   ALU.subtract).then_inc(ln_centered, 1)

            def scale_tokens(g, i, u):
                pool.wait_ge(ln_centered, g + 1)
                pool.wait_ge(ln_rstd_ready, i + 2)
                tiles = slice(0, J - 1)
                pool.tensor_tensor(xln[:, u, tiles], xln[:, u, tiles],
                                   x_rstd[:, u, tiles].unsqueeze(2).to_broadcast([P, J - 1, D]),
                                   ALU.mult).then_inc(xln_ready, 1)

            def second_rstd(n, u):
                settled = held(pool, wait_count, n + G + 1)
                pool.wait_ge(vec_zeroed, 1)
                pool.wait_ge(ln_mv_step, settled)
                pool.tensor_scalar(x_var[:, u], x_mv[:, u, :, 1], EPS, None, ALU.add).then_inc(ln_var_step, 1)
                pool.wait_ge(ln_var_step, n + 1)
                pool.tensor_tensor(x_rstd[:, u], x_var[:, u], minus_half[:, 0:J], ALU.pow).then_inc(ln_rstd_ready, 1)

            def batch_norm_rstd(at, mean_var, count, done):
                pool.wait_ge(bn_mv_ready, done)
                pool.tensor_scalar(bn_var[:, at:at + count], mean_var, EPS, None, ALU.add).then_inc(bn_var_step, 1)
                pool.wait_ge(bn_var_step, done)
                pool.tensor_tensor(bn_rstd[:, at:at + count], bn_var[:, at:at + count], minus_half[:, 0:count],
                                   ALU.pow).then_inc(bn_rstd_ready, 1)

            def norm_turn(i):
                first_rstd(i)
                for u in range(2):
                    center_tokens(i * 2 + u, u)
                    scale_tokens(i * 2 + u, i, u)

            for u in range(2):
                pool.wait_ge(gnn_mv_ready, u + 1)
                pool.tensor_tensor(start_rstd[:, u], gnn_mv[:, u, :, 1], minus_half[:, 0:J],
                                   ALU.pow).then_inc(ln_rstd_ready, 1)
                center_tokens(u, u)
            norm_turn(1)
            with pool.Fori(2, PAIRS) as i:
                norm_turn(i)

            batch_norm_rstd(0, h_mv[:, :, 1], HT, 1)
            pool.wait_ge(fw_loaded, 64)
            for a, b in ((0, W1C), (W1C, W1C + W2C)):
                pool.tensor_copy(fw_hi[:, a:b], fw_raw[:, a:b]).then_inc(fw_split, 1)
            pool.wait_ge(fw_split, 2)
            for a, b in ((0, W1C), (W1C, W1C + W2C)):
                pool.tensor_tensor(fw_lo[:, a:b], fw_raw[:, a:b], fw_hi[:, a:b].bitcast(F32),
                                   ALU.subtract).then_inc(fw_split, 1)
            batch_norm_rstd(HT, y_mv[:, 1:2], 1, 2)

            def norm_x(n, u):
                second_rstd(n, u)
                settled = held(pool, wait_count, n)
                pool.wait_ge(vec_zeroed, 1)
                pool.wait_ge(xt_done, settled)
                pool.tensor_tensor(x_norm, group_tiles(n), x_mv[:, u, :, 0:1].to_broadcast([P, J, D]),
                                   ALU.subtract).then_inc(ln_centered, 1)
                pool.wait_ge(ln_centered, n + G)
                pool.wait_ge(ln_rstd_ready, n + PAIRS + 2)
                pool.tensor_tensor(x_norm, x_norm, x_rstd[:, u].unsqueeze(2).to_broadcast([P, J, D]),
                                   ALU.mult).then_inc(x_normed, 1)

            second_rstd(0, 0)
            norm_x(1, 1)

            def turn(i, last=False):
                for u in range(2):
                    g = i * 2 + u
                    for e in range(E):
                        if e == 1 and not last:
                            norm_x(g + 2, u)
                        if e >= 1 and not (last and u == 1 and e >= E - 2):
                            pool.wait_ge(masked, g * E + e + 1)
                            pool.wait_ge(added, from_zero(g * (E - 1) + e - 1))
                            pool.tensor_tensor(ffn_sum[:, u], ffn_sum[:, u], y_masked[:, e % 2],
                                               ALU.add).then_inc(added, 1)

            turn(0)
            with pool.Fori(1, PAIRS - 1) as i:
                turn(i)
            turn(PAIRS - 1, last=True)

        @block.scalar
        def _(act):
            def evacuate_hidden(g, u):
                act.wait_ge(h1_done, g + 1)
                for k in range(HT):
                    act.activation(group_columns(h1[:, k, :], g), h1_ps[:, u, k, :], ACT.Identity,
                                   bias=column("gb1", k)).then_inc(h1_ready, 1)

            def scale_tiles(g, i, u, first, rstd=x_rstd):
                act.wait_ge(ln_centered, g + 1)
                act.wait_ge(ln_rstd_ready, i + 2)
                for j in range(first, J):
                    ins = act.activation(xln[:, u, j, :], xln[:, u, j, :], ACT.Identity, scale=rstd[:, u, j:j + 1])
                ins.then_inc(act_scaled, 1)

            def round_aggregate(g, u):
                act.wait_ge(agg_done, g + 1)
                act.wait_ge(h1_done, from_zero(g - 1))
                act.copy(agg_hi[:, u], agg_ps[:, u]).then_inc(agg_hi_ready, 1)

            act.dma_start(gw1_raw, gw1.rearrange("(k p) d -> p k d", p=P)).then_inc(gw_loaded, 16)
            act.dma_start(gw2_raw, gw2).then_inc(gw_loaded, 16)
            act.wait_ge(dinv_ready, 1)
            act.wait_ge(adj_step, 4)
            for k in range(KT):
                act.activation(adj_sb[:, k, :], adj_sb[:, k, :], ACT.Identity,
                               scale=dinv[:, k:k + 1]).then_inc(adj_scaled, 1)
            act.wait_ge(adj_turned, 1)
            for k in range(KT):
                act.activation(a_t[:, k, :], work_b[:, k * N:(k + 1) * N], ACT.Identity,
                               scale=dinv[:, k:k + 1]).then_inc(a_t_ready, 1)
            scale_tiles(0, -1, 0, 0, start_rstd)
            act.wait_ge(weights_turned, 1)
            act.copy(gw1_hi[:], weights_ps[:, 0:HT, :]).then_inc(weights_ready, 1)
            act.copy(gw2_t[:], weights_ps[:, HT:2 * HT, :]).then_inc(weights_ready, 1)
            scale_tiles(1, 0, 1, 0, start_rstd)
            round_aggregate(0, 0)
            round_aggregate(1, 1)
            scale_tiles(2, 1, 0, J - 1)
            act.wait_ge(weights_turned, 2)
            act.copy(vec[:], h1_ps[:, 0, 0, 0:P]).then_inc(weights_ready, 1)
            act.wait_ge(weights_ready, 3)

            def gnn_turn(i, last=False):
                for u in range(2):
                    g = i * 2 + u
                    if not (last and u == 1):
                        scale_tiles(g + 3, i + 1 + u, 1 - u, J - 1)
                    round_aggregate(g + 2, u)
                    evacuate_hidden(g, u)

            with act.Fori(0, PAIRS - 2) as i:
                gnn_turn(i)
            gnn_turn(PAIRS - 2, last=True)
            evacuate_hidden(G - 2, 0)
            evacuate_hidden(G - 1, 1)

            act.wait_ge(bn_ready, 1)

            def relu(i):
                for u in range(2):
                    g = i * 2 + u
                    act.wait_ge(y_done, from_zero(g - 1))
                    for k in range(HT):
                        act.activation(h_relu[:, u, k, :], group_columns(h1[:, k, :], g), ACT.Relu,
                                       bias=bn_shift[:, k:k + 1], scale=bn_scale[:, k:k + 1]).then_inc(relu_done, 1)

            relu(0)
            with act.Fori(1, PAIRS) as i:
                relu(i)

            def split_hi_x(n, u):
                act.wait_ge(xt_done, n + 1)
                act.copy(xt_hi[:, u], work_b).then_inc(xt_hi_ready, 1)

            split_hi_x(0, 0)

            def turn(i, first=False, last=False):
                for u in range(2):
                    g = i * 2 + u
                    for e in range(E):
                        q = g * E + e
                        r = e % RING
                        for f in range(FT):
                            act.wait_ge(up_done, q * FT + f + 1)
                            if f == 0:
                                act.wait_ge(lo_done, from_zero(q - RING + 1))
                            act.activation(hid[:, r, f, :], hid_ps[:, e % 2, f, :], ACT.Gelu,
                                           bias=column("fb1", e * FT + f)).then_inc(gelu_done, 1)
                        act.wait_ge(gelu_done, (q + 1) * FT)
                        act.wait_ge(down_done, from_zero(q - RING + 1))
                        act.copy(hid_hi[:, r], hid[:, r]).then_inc(hi_done, 1)
                        if e == (2 if first and u == 0 else 1) and not (last and u == 1):
                            split_hi_x(g + 1, 1 - u)

            turn(0, first=True)
            with act.Fori(1, PAIRS - 1) as i:
                turn(i)
            turn(PAIRS - 1, last=True)

        @block.vector
        def _(dve):
            wait_count = ctx.enter_context(dve.register("wait_count"))
            dve.wait_ge(const_ready, 5)
            dve.wait_ge(adj_loaded, 16)
            dve.tensor_tensor(adj_sb[:], adj_sb[:], eye[:], ALU.add).then_inc(adj_step, 1)
            dve.wait_ge(adj_step, 1)
            dve.tensor_reduce(row_sum[:], adj_sb[:], AX_X, ALU.add).then_inc(adj_step, 1)
            dve.tensor_tensor(eye_adj[:], adj_sb[:], eye[:], ALU.mult).then_inc(adj_step, 1)
            dve.wait_ge(adj_step, 3)
            dve.tensor_reduce(diag[:], eye_adj[:], AX_X, ALU.add).then_inc(adj_step, 1)
            dve.wait_ge(col_sum_done, 1)
            dve.tensor_tensor(deg[:], work_a[:, 0:KT], row_sum[:], ALU.add).then_inc(adj_step, 1)
            dve.wait_ge(adj_step, 5)
            dve.tensor_tensor(deg[:], deg[:], diag[:], ALU.subtract).then_inc(deg_ready, 1)

            def tile_stats(g, u):
                tiles = group_tiles(g)
                for j in range(J):
                    ins = dve.bn_stats(x_stats[:, u, j, :], tiles[:, j, :])
                ins.then_inc(ln_stats_step, 1)

            def tile_means(n, u):
                settled = held(dve, wait_count, n + 1)
                dve.wait_ge(vec_zeroed, 1)
                dve.wait_ge(ln_stats_step, settled)
                for j in range(J):
                    ins = dve.bn_aggr(x_mv[:, u, j, :], x_stats[:, u, j, :])
                ins.then_inc(ln_mv_step, 1)

            def keep_means(g, u):
                dve.wait_ge(ln_mv_step, g + 1)
                dve.tensor_tensor(gnn_mv[:, bass.ds(g, 1), :, :].rearrange("p a j m -> p (a j) m"), x_mv[:, u],
                                  zero_eps[:], ALU.add).then_inc(gnn_mv_ready, 1)

            def first_norm_stats(g, u):
                tile_stats(g, u)
                tile_means(g, u)
                keep_means(g, u)

            def hidden_stats(g):
                settled = held(dve, wait_count, g * HT + HT)
                dve.wait_ge(vec_zeroed, 1)
                dve.wait_ge(h1_ready, settled)
                for k in range(HT):
                    ins = dve.bn_stats(h_stats[:, k, bass.ds(g, 1), :].rearrange("p a s -> p (a s)"),
                                       group_columns(h1[:, k, :], g))
                ins.then_inc(h1_counted, 1)

            dve.wait_ge(x_load[0], 16)
            first_norm_stats(0, 0)
            first_norm_stats(1, 1)
            dve.wait_ge(x_load[1], 16)
            first_norm_stats(2, 0)
            first_norm_stats(3, 1)
            dve.wait_ge(x_loaded, AHEAD)
            for g in range(4, AHEAD):
                first_norm_stats(g, g % 2)

            def split_lo_aggregate(g, u):
                dve.wait_ge(agg_hi_ready, g + 1)
                dve.wait_ge(h1_done, from_zero(g - 1))
                dve.tensor_tensor(agg_lo[:, u], agg_ps[:, u], agg_hi[:, u].bitcast(F32),
                                  ALU.subtract).then_inc(agg_lo_ready, 1)

            def gnn_turn(i):
                for u in range(2):
                    g = i * 2 + u
                    more = not (isinstance(g, int) and g + AHEAD >= G)
                    start = isinstance(g, int) and g == 0
                    if start:
                        split_lo_aggregate(0, 0)
                        dve.wait_ge(weights_ready, 2)
                        dve.tensor_tensor(gw1_lo[:], weights_ps[:, 0:HT, :], gw1_hi[:].bitcast(F32),
                                          ALU.subtract).then_inc(gw1_lo_ready, 1)
                    if more:
                        settled = held(dve, wait_count, g + AHEAD + 1)
                        dve.wait_ge(vec_zeroed, 1)
                        dve.wait_ge(x_loaded, settled)
                        tile_stats(g + AHEAD, u)
                    if not start:
                        split_lo_aggregate(g, u)
                    if more:
                        tile_means(g + AHEAD, u)
                    if not (isinstance(g, int) and (g < 3 or g == G - 1)):
                        hidden_stats(g - 3)
                    if more:
                        keep_means(g + AHEAD, u)
                    if isinstance(g, int) and g >= G - 2:
                        hidden_stats(g - 2)

            gnn_turn(0)
            gnn_turn(1)
            with dve.Fori(2, PAIRS - AHEAD // 2) as i:
                gnn_turn(i)
            for i in range(PAIRS - AHEAD // 2, PAIRS - 1):
                gnn_turn(i)
            gnn_turn(PAIRS - 1)
            hidden_stats(G - 2)
            for k in range(HT):
                dve.wait_ge(h1_ready, (G - 1) * HT + k + 1)
                ins = dve.bn_stats(h_stats[:, k, G - 1, :], group_columns(h1[:, k, :], G - 1))
            ins.then_inc(h1_counted, 1)

            def batch_norm(at, count, mean, gamma, beta, done):
                dve.wait_ge(bn_rstd_ready, done)
                c = slice(at, at + count)
                dve.tensor_tensor(bn_scale[:, c], bn_rstd[:, c], gamma, ALU.mult).then_inc(bn_step, 1)
                dve.wait_ge(bn_step, from_zero(2 * done - 1))
                dve.tensor_tensor(bn_mean_scaled[:, c], mean, bn_scale[:, c], ALU.mult).then_inc(bn_step, 1)
                dve.wait_ge(bn_step, 2 * done)
                dve.tensor_tensor(bn_shift[:, c], beta, bn_mean_scaled[:, c], ALU.subtract).then_inc(bn_ready, 1)

            dve.wait_ge(h1_counted, G)
            for k in range(HT):
                ins = dve.bn_aggr(h_mv[:, k, :], h_stats[:, k].rearrange("p g s -> p (g s)"))
            ins.then_inc(bn_mv_ready, 1)
            batch_norm(0, HT, h_mv[:, :, 0], vec[:, names["gg1"]:names["gg1"] + HT],
                       vec[:, names["gbe1"]:names["gbe1"] + HT], 1)
            dve.wait_ge(fw_loaded, 64)
            dve.tensor_copy(wg_parts[:, 0, :], wg_raw[:]).then_inc(wg_split, 1)
            dve.wait_ge(wg_split, 1)
            dve.tensor_tensor(wg_parts[:, 1, :], wg_raw[:], wg_parts[:, 0, :].bitcast(F32),
                              ALU.subtract).then_inc(wg_split, 1)

            with dve.Fori(0, PAIRS) as i:
                for u in range(2):
                    g = i * 2 + u
                    dve.wait_ge(y_done, g + 1)
                    dve.tensor_scalar(group_columns(y, g), y_ps[:, u], column("gb2"), None,
                                      ALU.add).then_inc(y_ready, 1)
                    settled = held(dve, wait_count, g + 1)
                    dve.wait_ge(vec_zeroed, 1)
                    dve.wait_ge(y_ready, settled)
                    dve.bn_stats(y_stats[:, bass.ds(g, 1), :].rearrange("p a s -> p (a s)"),
                                 group_columns(y, g)).then_inc(y_counted, 1)
            dve.wait_ge(y_counted, G)
            dve.bn_aggr(y_mv[:], y_stats[:].rearrange("p g s -> p (g s)")).then_inc(bn_mv_ready, 1)
            batch_norm(HT, 1, y_mv[:, 0:1], column("gg2"), column("gbe2"), 2)
            dve.wait_ge(bn_ready, 2)

            def norm_y(n):
                dve.wait_ge(y_turned, from_zero(n))
                dve.tensor_scalar(y_norm, group_columns(y, n), bn_scale[:, HT:HT + 1], bn_shift[:, HT:HT + 1],
                                  ALU.mult, ALU.add).then_inc(y_normed, 1)

            def add_residual(n):
                dve.wait_ge(y_turned, n + 1)
                tiles = group_tiles(n)
                dve.tensor_tensor(tiles, work_a.rearrange("p (j d) -> p j d", j=J), tiles, ALU.add).then_inc(x2_ready, 1)

            def second_norm_stats(n, u):
                settled = held(dve, wait_count, n + 1)
                dve.wait_ge(vec_zeroed, 1)
                dve.wait_ge(x2_ready, settled)
                tile_stats(n, u)
                tile_means(n + G, u)

            def norm_first_x():
                dve.wait_ge(ln_rstd_ready, PAIRS + 2)
                for j in range(J):
                    dve.tensor_scalar(x_norm[:, j, :], x_sb[:, j, :], x_mv[:, 0, j, 0:1], x_rstd[:, 0, j:j + 1],
                                      ALU.subtract, ALU.mult).then_inc(first_x_normed, 1)

            def split_lo_x(n, u):
                dve.wait_ge(xt_hi_ready, n + 1)
                dve.tensor_tensor(xt_lo[:, u], work_b, xt_hi[:, u].bitcast(F32), ALU.subtract).then_inc(xt_lo_ready, 1)

            def pick_experts(n):
                dve.wait_ge(gate_done, n + 1)
                scores = work_a[:, 0:J * 2 * E].rearrange("p (j h e) -> p j h e", j=J, h=2)
                bias = bg_sb[:].unsqueeze(1).to_broadcast([P, J, E])
                dve.tensor_tensor(gate[:], scores[:, :, 0, :], bias, ALU.add).then_inc(gate_step, 1)
                dve.wait_ge(gate_step, n * PICK_STEPS + 1)
                dve.tensor_tensor(gate[:], scores[:, :, 1, :], gate[:], ALU.add).then_inc(gate_step, 1)
                settled = held(dve, wait_count, n * PICK_STEPS + 2)
                dve.wait_ge(vec_zeroed, 1)
                dve.wait_ge(gate_step, settled)
                for j in range(J):
                    ins = dve.max(gate_max[:, j, :], gate[:, j, :])
                ins.then_inc(gate_step, 1)
                settled = held(dve, wait_count, n * PICK_STEPS + 3)
                dve.wait_ge(vec_zeroed, 1)
                dve.wait_ge(gate_step, settled)
                for j in range(J):
                    ins = dve.max_index(gate_idx[:, j, :], gate_max[:, j, :], gate[:, j, :])
                ins.then_inc(gate_step, 1)
                dve.wait_ge(gate_step, n * PICK_STEPS + 4)
                for k in range(2):
                    ins = dve.tensor_tensor(picked[:, k], expert_number[:],
                                            gate_idx[:, :, k:k + 1].to_broadcast([P, J, E]), ALU.is_equal)
                ins.then_inc(gate_step, 1)
                dve.wait_ge(gate_step, n * PICK_STEPS + 5)
                dve.wait_ge(mask_turned, from_zero(n))
                dve.tensor_tensor(mask[:].rearrange("p e j -> p j e"), picked[:, 0], picked[:, 1],
                                  ALU.add).then_inc(mask_ready, 1)

            def copy_mask(n):
                dve.wait_ge(mask_turned, n + 1)
                dve.wait_ge(mask_stored, from_zero(n * 16))
                dve.tensor_copy(mask_t[:], work_a[0:E * J, 0:P]).then_inc(mask_t_ready, 1)

            def mask_expert(g, e, i, u):
                q = g * E + e
                dve.wait_ge(down_done, q + 1)
                if e == 0:
                    dve.wait_ge(mask_loaded[u], i * 16 + 16)
                    dve.wait_ge(sum_turned, from_zero(g - 1))
                    target = ffn_sum[:, u]
                else:
                    dve.wait_ge(added, from_zero(g * (E - 1) + (e - 2 if e > 2 else 0)))
                    target = y_masked[:, e % 2]
                dve.scalar_tensor_tensor(out=target, in0=ffn_ps[:, e % 2], scalar=column("fb2", e),
                                         in1=mask_bc[:, u, e, :], op0=ALU.add, op1=ALU.mult).then_inc(masked, 1)

            def split_lo_hidden(g, e):
                q = g * E + e
                dve.wait_ge(hi_done, q + 1)
                dve.wait_ge(down_done, from_zero(q - RING + 1))
                r = e % RING
                dve.tensor_tensor(hid_lo[:, r], hid[:, r], hid_hi[:, r].bitcast(F32),
                                  ALU.subtract).then_inc(lo_done, 1)

            def finish(o, i, u, source):
                dve.wait_ge(sum_turned, o + 1)
                dve.wait_ge(out_stored[u], from_zero(i * 16))
                dve.tensor_tensor(out_sb[:, u], source, group_tiles(o), ALU.add).then_inc(out_ready, 1)

            norm_y(0)
            add_residual(0)
            second_norm_stats(0, 0)
            norm_y(1)
            norm_first_x()
            add_residual(1)
            split_lo_x(0, 0)
            second_norm_stats(1, 1)

            def turn(i, first=False, last=False):
                for u in range(2):
                    g = i * 2 + u
                    start = first and u == 0
                    prepare = not (last and u == 1)
                    for e in range(E):
                        if e == LAG and start:
                            second_norm_stats(2, 0)
                            split_lo_hidden(0, LAG)
                        if e >= LAG:
                            mask_expert(g, e - LAG, i, u)
                        elif not start:
                            mask_expert(g - 1, E - LAG + e, i if u else i - 1, 1 - u)
                        if e == 0 and not last:
                            norm_y(g + 2)
                        if e == 2 and not last:
                            add_residual(g + 2)
                        if e == 3 and not last and not start:
                            second_norm_stats(g + 2, u)
                        if e == 4 and prepare:
                            pick_experts(g + 1)
                        if e == 5 and not start:
                            finish(g - 1, i if u else i - 1, 1 - u, work_b.rearrange("p (j d) -> p j d", j=J))
                        if e == 6 and prepare:
                            copy_mask(g + 1)
                        if e == 0 and start:
                            pick_experts(0)
                        if e == 1 and start:
                            copy_mask(0)
                        if not (e == LAG and start):
                            split_lo_hidden(g, e)
                        if e == (2 if start else 1) and prepare:
                            split_lo_x(g + 1, 1 - u)

            turn(0, first=True)
            with dve.Fori(1, PAIRS - 1) as i:
                turn(i)
            turn(PAIRS - 1, last=True)
            for e in range(E - LAG, E):
                mask_expert(G - 1, e, PAIRS - 1, 1)
            finish(G - 1, PAIRS - 1, 1, last_out_ps)

        @block.tensor
        def _(pe):
            def turn_tiles(target, source, count):
                for j in range(count):
                    ins = pe.transpose(target[:, j * P:(j + 1) * P], source(j), ident[:])
                return ins

            def keep_clock_up(count, bank):
                for _ in range(count):
                    pe.matmul(bank, ident_bf[:], eye_bf, start=True, stop=True)

            pe.wait_ge(const_ready, 18)
            pe.wait_ge(adj_step, 1)
            for k in range(KT):
                for l in range(KT):
                    ins = pe.matmul(work_a[:, k:k + 1], adj_sb[:, l, k::KT], ones[:, 0:1],
                                    start=(l == 0), stop=(l == KT - 1))
            ins.then_inc(col_sum_done, 1)
            keep_clock_up(6, agg_ps[:, 0])
            pe.wait_ge(adj_scaled, KT)
            ins = turn_tiles(work_b, lambda c: adj_sb[:, c % KT, (c // KT)::KT], KT * KT)
            ins.then_inc(adj_turned, 1)
            pe.wait_ge(gw_loaded, 32)
            ins = turn_tiles(h1_ps[:, 0, 1, :],
                             lambda c: gw1_raw[:, c, :] if c < HT else gw2_raw[:, (c - HT) * P:(c - HT + 1) * P], 2 * HT)
            ins.then_inc(weights_turned, 1)
            keep_clock_up(6, agg_ps[:, 0])
            pe.wait_ge(a_t_ready, KT)

            def aggregate(g, u):
                pe.wait_ge(xln_ready, from_zero(g - 1))
                pe.wait_ge(act_scaled, g + 1)
                pe.wait_ge(agg_lo_ready, from_zero(g - 1))
                for b in range(BG):
                    for k in range(KT):
                        ins = pe.matmul(agg_ps[:, u, b * N:(b + 1) * N], xln[:, u, b * KT + k, :], a_t[:, k, :],
                                        start=(k == 0), stop=(k == KT - 1))
                ins.then_inc(agg_done, 1)

            def hidden(g, u):
                pe.wait_ge(agg_lo_ready, g + 1)
                pe.wait_ge(h1_ready, from_zero((g - 1) * HT))
                for k in range(HT):
                    o = h1_ps[:, u, k, :]
                    pe.matmul(o, gw1_hi[:, k, :], agg_hi[:, u], start=True, stop=False)
                    pe.matmul(o, gw1_hi[:, k, :], agg_lo[:, u], start=False, stop=False)
                    ins = pe.matmul(o, gw1_lo[:, k, :], agg_hi[:, u], start=False, stop=True)
                ins.then_inc(h1_done, 1)

            aggregate(0, 0)
            aggregate(1, 1)
            pe.wait_ge(vec_loaded, 8 * 16)
            pe.transpose(h1_ps[:, 0, 0, 0:P], vec_rows[:], ident[:]).then_inc(weights_turned, 1)
            aggregate(2, 0)
            pe.wait_ge(weights_ready, 3)
            pe.wait_ge(gw1_lo_ready, 1)
            hidden(0, 0)
            aggregate(3, 1)
            hidden(1, 1)
            with pe.Fori(1, PAIRS - 1) as i:
                for u in range(2):
                    aggregate(i * 2 + 2 + u, u)
                    hidden(i * 2 + u, u)
            hidden(G - 2, 0)
            hidden(G - 1, 1)

            keep_clock_up(23, agg_ps[:, 0])

            def second_layer(i):
                for u in range(2):
                    g = i * 2 + u
                    pe.wait_ge(y_ready, from_zero(g - 1))
                    for k in range(HT):
                        pe.wait_ge(relu_done, g * HT + k + 1)
                        ins = pe.matmul(y_ps[:, u], gw2_t[:, k, :], h_relu[:, u, k, :],
                                        start=(k == 0), stop=(k == HT - 1))
                    ins.then_inc(y_done, 1)

            second_layer(0)
            with pe.Fori(1, PAIRS) as i:
                second_layer(i)

            def turn_y(n):
                pe.wait_ge(y_normed, n + 1)
                if isinstance(n, int) and n < 2:
                    pe.wait_ge(x2_ready, n)
                else:
                    pe.wait_ge(mask_t_ready, n - 1)
                turn_tiles(work_a, lambda j: y_norm[:, j * P:(j + 1) * P], J).then_inc(y_turned, 1)

            def turn_first_x():
                for j in range(J):
                    pe.wait_ge(first_x_normed, j + 1)
                    ins = pe.transpose(work_b[:, j * P:(j + 1) * P], x_norm[:, j, :], ident[:])
                ins.then_inc(xt_done, 1)

            def turn_x(n):
                pe.wait_ge(x_normed, n)
                pe.wait_ge(out_ready, from_zero(n - 2))
                turn_tiles(work_b, lambda j: x_norm[:, j, :], J).then_inc(xt_done, 1)

            def gate_scores(n, u):
                pe.wait_ge(xt_lo_ready, n + 1)
                pe.wait_ge(x2_ready, min(n + 2, G) if isinstance(n, int) else n + 2)
                parts = wg_parts[:].rearrange("p h e -> p (h e)")
                for j in range(J):
                    c = slice(j * P, (j + 1) * P)
                    o = work_a[:, j * 2 * E:(j + 1) * 2 * E]
                    pe.matmul(o, xt_hi[:, u, c], parts, start=True, stop=False)
                    ins = pe.matmul(o, xt_lo[:, u, c], parts, start=False, stop=True)
                ins.then_inc(gate_done, 1)

            def turn_mask(n):
                pe.wait_ge(mask_ready, n + 1)
                pe.matmul(work_a[0:E * J, 0:P], mask[:].rearrange("p e j -> p (e j)"), ident_bf[:],
                          start=True, stop=True).then_inc(mask_turned, 1)

            def turn_sum(o, u):
                pe.wait_ge(added, (o + 1) * (E - 1))
                if isinstance(o, int) and o == G - 2:
                    pe.wait_ge(out_ready, G - 2)
                else:
                    pe.wait_ge(xt_lo_ready, o + 3)
                turn_tiles(work_b, lambda j: ffn_sum[:, u, j * P:(j + 1) * P], J).then_inc(sum_turned, 1)

            def turn_last_sum():
                def turn_and_add(source, first=False, last=False):
                    for j in range(J):
                        c = slice(j * P, (j + 1) * P)
                        ins = pe.matmul(last_out_ps[:, j, :], source[:, c], ident[:], start=first, stop=last)
                    return ins

                pe.wait_ge(gelu_done, G * E * FT)
                pe.wait_ge(added, G * (E - 1) - 2)
                turn_and_add(ffn_sum[:, 1], first=True)
                pe.wait_ge(masked, G * E - 1)
                turn_and_add(y_masked[:, E % 2])
                pe.wait_ge(masked, G * E)
                turn_and_add(y_masked[:, (E - 1) % 2], last=True).then_inc(sum_turned, 1)

            def up(g, e, u):
                q = g * E + e
                if e == 0:
                    pe.wait_ge(xt_hi_ready, g + 1)
                pe.wait_ge(gelu_done, from_zero((q - 1) * FT))
                for f in range(FT):
                    o = hid_ps[:, e % 2, f, :]
                    pe.matmul(o, w1(fw_hi, e, f), xt_hi[:, u], start=True, stop=False)
                    pe.matmul(o, w1(fw_lo, e, f), xt_hi[:, u], start=False, stop=False)
                    if e == 0 and f == 0:
                        pe.wait_ge(xt_lo_ready, g + 1)
                    pe.matmul(o, w1(fw_hi, e, f), xt_lo[:, u], start=False, stop=True).then_inc(up_done, 1)

            def down(g, e):
                q = g * E + e
                pe.wait_ge(lo_done, q + 1)
                pe.wait_ge(masked, from_zero(q - 1))
                o = ffn_ps[:, e % 2]
                for f in range(FT):
                    pe.matmul(o, w2(fw_hi, e, f), hid_hi[:, e % RING, f, :], start=(f == 0), stop=False)
                    pe.matmul(o, w2(fw_hi, e, f), hid_lo[:, e % RING, f, :], start=False, stop=False)
                    ins = pe.matmul(o, w2(fw_lo, e, f), hid_hi[:, e % RING, f, :], start=False, stop=(f == FT - 1))
                ins.then_inc(down_done, 1)

            keep_clock_up(19, ffn_ps[:, 1])
            turn_y(0)
            keep_clock_up(9, ffn_ps[:, 1])
            turn_y(1)
            keep_clock_up(4, ffn_ps[:, 1])
            turn_first_x()
            keep_clock_up(6, ffn_ps[:, 1])
            pe.wait_ge(wg_split, 2)
            pe.wait_ge(fw_split, 4)

            def turn(i, first=False, last=False):
                for u in range(2):
                    g = i * 2 + u
                    start = first and u == 0
                    prepare = not (last and u == 1)
                    for e in range(E):
                        up(g, e, u)
                        if e == 0 and start:
                            gate_scores(0, 0)
                        if e == 2 and start:
                            turn_mask(0)
                        if e == 3 and not last:
                            turn_y(g + 2)
                        if e == (2 if start else 1) and prepare:
                            turn_x(g + 1)
                        if e == 4 and prepare:
                            gate_scores(g + 1, 1 - u)
                        if e == 4 and not start:
                            turn_sum(g - 1, 1 - u)
                        if e == 6 and prepare:
                            turn_mask(g + 1)
                        if e >= LAG:
                            down(g, e - LAG)
                        elif not start:
                            down(g - 1, E - LAG + e)

            turn(0, first=True)
            with pe.Fori(1, PAIRS - 1) as i:
                turn(i)
            turn(PAIRS - 1, last=True)
            for e in range(E - LAG, E):
                down(G - 1, e)
            turn_last_sum()


_INS = ["x", "adj", "L0_gnn_W1", "L0_gnn_b1", "L0_gnn_g1", "L0_gnn_be1", "L0_gnn_W2", "L0_gnn_b2", "L0_gnn_g2",
        "L0_gnn_be2", "L0_ffn_Wg", "L0_ffn_bg", "L0_ffn_W1", "L0_ffn_b1", "L0_ffn_W2", "L0_ffn_b2"]


def kernel(**inputs):
    import numpy as _np
    import concourse.bacc as _bacc
    from concourse import mybir as _mybir
    from concourse.bass_utils import run_bass_kernel_spmd as _run

    nc = _bacc.Bacc("TRN2", target_bir_lowering=False, num_devices=1)
    arrays, args = {}, []
    for name in _INS:
        a = _np.ascontiguousarray(inputs[name])
        arrays[f"in_{name}_dram"] = a
        args.append(nc.dram_tensor(f"in_{name}_dram", a.shape, _mybir.dt.from_np(a.dtype), kind="ExternalInput").ap())
    shape = inputs["x"].shape
    out = nc.dram_tensor("out_0_dram", shape, _mybir.dt.float32, kind="ExternalOutput").ap()
    gnn_moe_program(nc, *args, out)
    r = _run(nc, [arrays], core_ids=[0])
    return r.results[0]["out_0_dram"]
```
